# Optimizing a Trainium2 kernel written in Bass

```python
import numpy as np
import jax
import jax.numpy as jnp

def _softmax(x, axis=-1):
    return jax.nn.softmax(x, axis=axis)

def _gelu(x):
    return jax.nn.gelu(x, approximate=True)

def _silu(x):
    return jax.nn.silu(x)

def _sigmoid(x):
    return jax.nn.sigmoid(x)

def _layernorm(x, axis=-1, eps=1e-05):
    m = jnp.mean(x, axis=axis, keepdims=True)
    v = jnp.var(x, axis=axis, keepdims=True)
    return (x - m) / jnp.sqrt(v + eps)

def _scatter_add(tgt, idx, src, axis=0):
    return tgt.at[idx].add(src)

def _segment_sum(src, seg, n):
    return jax.ops.segment_sum(src, seg, n)
kernel_name = 'mk_xattn_ffn_d1_seqx_r2_a7ca2d'

def setup_inputs(seed: int=0):
    np.random.seed(seed)
    _w = jnp.asarray

    def _rec_inputs():
        import jax
        import jax.numpy as jnp
        _rk = jax.random.key(seed)
        x = 7.22e-05 + 1 * jax.random.normal(jax.random.fold_in(_rk, 1), (4, 1024, 512), jnp.float32)
        _lenS = 1024 - jax.random.randint(jax.random.fold_in(_rk, 7), (4,), 0, max(1, 1024 // 4) + 1, jnp.int32)
        _lenS2 = 2048 - jax.random.randint(jax.random.fold_in(_rk, 8), (4,), 0, max(1, 2048 // 4) + 1, jnp.int32)
        _ctx_1024P = jax.random.normal(jax.random.fold_in(_rk, 11), (4, 16, 512), jnp.float32)
        _ctx_1024c = jax.random.dirichlet(jax.random.fold_in(_rk, 511), 0.3 * jnp.ones((16,), jnp.float32), (4, 2048))
        _ctx_1024t = jnp.einsum('bsk,bkd->bsd', _ctx_1024c, _ctx_1024P)
        _ctx_1024t = _ctx_1024t * jax.lax.rsqrt(jnp.mean(jnp.square(_ctx_1024t)) + 1e-12) * 0.953939
        ctx_1024 = 4.13588e-05 + 0.999923 * (_ctx_1024t + 0.3 * jax.random.normal(jax.random.fold_in(_rk, 611), (4, 2048, 512), jnp.float32))
        _validS = jnp.arange(1024)[None, :] < _lenS[:, None]
        _validS2 = jnp.arange(2048)[None, :] < _lenS2[:, None]
        _causal = jnp.tril(jnp.ones((1024, 1024), dtype=bool))
        mask_Bx1x1xS2_ik0 = jnp.where(jnp.broadcast_to(_validS2[:, None, None, :], (4, 1, 1, 2048)), 0, 1).astype(jnp.int32)
        return (x, ctx_1024, mask_Bx1x1xS2_ik0)
    x, ctx_1024, mask_Bx1x1xS2_ik0 = _rec_inputs()

    def _L0_xattn_setup():
        import jax, jax.numpy as jnp
        import numpy as np
        D_MODEL = 512
        N_HEADS = 16
        D_K = D_MODEL // N_HEADS
        B, T = (4, 1024)

        def _split_heads(x):
            b, t, _ = x.shape
            return x.reshape(b, t, N_HEADS, D_K).transpose(0, 2, 1, 3)
        key = jax.random.key(seed)
        ks = jax.random.split(key, 13)
        s = 1.0 / np.sqrt(D_MODEL)
        inp = {'Q': jax.random.normal(ks[0], (B, T, D_MODEL), jnp.float32), 'K': jax.random.normal(ks[1], (B, T, D_MODEL), jnp.float32), 'V': jax.random.normal(ks[2], (B, T, D_MODEL), jnp.float32), 'mask': jax.random.randint(ks[3], (B, 1, 1, T), 0, 2, jnp.int32), 'W_q': jax.random.normal(ks[4], (D_MODEL, D_MODEL), jnp.float32) * s, 'b_q': jax.random.normal(ks[5], (D_MODEL,), jnp.float32) * s, 'W_k': jax.random.normal(ks[6], (D_MODEL, D_MODEL), jnp.float32) * s, 'b_k': jax.random.normal(ks[7], (D_MODEL,), jnp.float32) * s, 'W_v': jax.random.normal(ks[8], (D_MODEL, D_MODEL), jnp.float32) * s, 'b_v': jax.random.normal(ks[9], (D_MODEL,), jnp.float32) * s, 'W_o': jax.random.normal(ks[10], (D_MODEL, D_MODEL), jnp.float32) * s, 'b_o': jax.random.normal(ks[11], (D_MODEL,), jnp.float32) * s}
        return inp
    _L0_xattn_all = _L0_xattn_setup()
    _L0_xattn_in = {k: v for k, v in _L0_xattn_all.items() if k in ('W_q', 'b_q', 'W_k', 'b_k', 'W_v', 'b_v', 'W_o', 'b_o')}
    del _L0_xattn_all

    def _L0_ffn_setup():
        import jax, jax.numpy as jnp
        import numpy as np
        D_MODEL = 512
        key = jax.random.key(seed)
        k_x, k_w, k_a1, k_a2 = jax.random.split(key, 4)
        x = jax.random.normal(k_x, (4, 1024, D_MODEL), dtype=jnp.float32)
        weight = jax.random.normal(k_w, (D_MODEL, D_MODEL), dtype=jnp.float32) * 0.02
        aux_weight1 = jax.random.normal(k_a1, (D_MODEL, D_MODEL), dtype=jnp.float32) * 0.02
        aux_weight2 = jax.random.normal(k_a2, (D_MODEL, D_MODEL), dtype=jnp.float32) * 0.02
        bias = jnp.zeros((D_MODEL,), dtype=jnp.float32)
        return {'x': x, 'weight': weight, 'aux_weight1': aux_weight1, 'aux_weight2': aux_weight2, 'bias': bias}
    _L0_ffn_all = _L0_ffn_setup()
    _L0_ffn_in = {k: v for k, v in _L0_ffn_all.items() if k in ('weight', 'aux_weight1', 'aux_weight2', 'bias')}
    del _L0_ffn_all
    return {'x': x, 'ctx_1024': ctx_1024, 'mask_Bx1x1xS2_ik0': mask_Bx1x1xS2_ik0, 'L0_xattn_W_q': _L0_xattn_in['W_q'], 'L0_xattn_b_q': _L0_xattn_in['b_q'], 'L0_xattn_W_k': _L0_xattn_in['W_k'], 'L0_xattn_b_k': _L0_xattn_in['b_k'], 'L0_xattn_W_v': _L0_xattn_in['W_v'], 'L0_xattn_b_v': _L0_xattn_in['b_v'], 'L0_xattn_W_o': _L0_xattn_in['W_o'], 'L0_xattn_b_o': _L0_xattn_in['b_o'], 'L0_ffn_weight': _L0_ffn_in['weight'], 'L0_ffn_aux_weight1': _L0_ffn_in['aux_weight1'], 'L0_ffn_aux_weight2': _L0_ffn_in['aux_weight2'], 'L0_ffn_bias': _L0_ffn_in['bias']}

def reference(x, ctx_1024, mask_Bx1x1xS2_ik0, L0_xattn_W_q, L0_xattn_b_q, L0_xattn_W_k, L0_xattn_b_k, L0_xattn_W_v, L0_xattn_b_v, L0_xattn_W_o, L0_xattn_b_o, L0_ffn_weight, L0_ffn_aux_weight1, L0_ffn_aux_weight2, L0_ffn_bias):
    import jax
    import jax.numpy as jnp

    def _L0_xattn_ref(Q, K, V, mask, W_q, b_q, W_k, b_k, W_v, b_v, W_o, b_o):
        import jax, jax.numpy as jnp
        import numpy as np
        D_MODEL = 512
        N_HEADS = 16
        D_K = D_MODEL // N_HEADS
        B, T = (4, 1024)

        def _split_heads(x):
            b, t, _ = x.shape
            return x.reshape(b, t, N_HEADS, D_K).transpose(0, 2, 1, 3)
        q = _split_heads(Q @ W_q.T + b_q)
        k = _split_heads(K @ W_k.T + b_k)
        v = _split_heads(V @ W_v.T + b_v)
        scale = 1.0 / jnp.sqrt(jnp.asarray(D_K, q.dtype))
        scores = jnp.einsum('bhqd,bhkd->bhqk', q, k) * scale
        scores = jnp.where(mask == 0, -jnp.inf, scores)
        attn = jax.nn.softmax(scores, axis=-1)
        out = jnp.einsum('bhqk,bhkd->bhqd', attn, v)
        bsz, h, t, dk = out.shape
        out = out.transpose(0, 2, 1, 3).reshape(bsz, t, h * dk)
        return out @ W_o.T + b_o

    def _L0_ffn_ref(x, weight, aux_weight1, aux_weight2, bias):
        import jax, jax.numpy as jnp
        import numpy as np
        D_MODEL = 512
        h = jnp.einsum('btc,cd->btd', x, weight)
        h = jnp.einsum('btc,cd->btd', h, aux_weight1)
        h = jnp.einsum('btc,cd->btd', h, aux_weight2)
        return jnp.tanh(h + bias)
    x = x + _L0_xattn_ref(_layernorm(x, axis=-1), ctx_1024, ctx_1024, mask_Bx1x1xS2_ik0, L0_xattn_W_q, L0_xattn_b_q, L0_xattn_W_k, L0_xattn_b_k, L0_xattn_W_v, L0_xattn_b_v, L0_xattn_W_o, L0_xattn_b_o)
    x = x + _L0_ffn_ref(_layernorm(x, axis=-1), L0_ffn_weight, L0_ffn_aux_weight1, L0_ffn_aux_weight2, L0_ffn_bias)
    return x

_drawn_inputs = setup_inputs


def setup_inputs(seed=0):
    import zlib

    import numpy as np

    out = dict(_drawn_inputs(seed))
    spreads = {'L0_ffn_bias': (0.0, 0.1)}
    factors = {'L0_xattn_b_q': 6.883, 'L0_xattn_b_k': 8.0}
    for name, (base, spread) in spreads.items():
        noise = np.random.default_rng([zlib.crc32(name.encode()), seed]).standard_normal(out[name].shape)
        drawn = base * np.exp(spread * noise) if base else spread * noise
        out[name] = jnp.asarray(drawn.astype(out[name].dtype))
    for name, factor in factors.items():
        out[name] = (out[name] * factor).astype(out[name].dtype)
    return out
```

```python
import numpy as np
import concourse.bass as bass
from concourse import mybir
from contextlib import ExitStack

B, T, S, D, H = 4, 1024, 2048, 512, 16
DK = D // H
P = 128
KC = D // P
HG = H // 4
NT = S // P
GT = 2
GK = GT * P
QH, QW = 2, 512
QT = T // P
EPS = 1e-5
SCALE = float(1.0 / np.sqrt(np.float32(DK)))
MASKED = -1.0e30
LOWEST = -3.0e38
NROW = 192
KB = 1024

DS = bass.ds


def control_constants():
    t = np.tile(np.arange(NT), B)
    b16 = np.repeat(np.arange(B) * NT, NT)
    ev = GT * np.arange(NT // GT)
    low = np.array([[1.0 if b < j else 0.0 for b in range(B)] for j in range(B + 1)]).ravel()
    row = np.zeros((1, NROW), np.float32)
    row[0, 156:160], row[0, 160:192] = np.arange(B), np.maximum(np.arange(32) - 1, 0)
    row[0, :64], row[0, 64:128], row[0, 128:136], row[0, 136:156] = t, b16, ev, low
    return row


def build(nc, x, ctx, mask, wq, bq, wk, bk, wv, bv, wo, bo, wf, wa1, wa2, fb, ident_in, rows_in, out):
    F32, F32R, I32 = mybir.dt.float32, mybir.dt.float32r, mybir.dt.int32
    ALU, ACT, AX = mybir.AluOpType, mybir.ActivationFunctionType, mybir.AxisListType.X

    x_rows = x.rearrange("b t d -> (b t) d")
    ctx_rows = ctx.rearrange("b t d -> (b t) d")
    out_rows = out.rearrange("b t d -> (b t) d")
    mask_rows = mask.rearrange("b u v (t p) -> (b u v t) p", p=P)
    mbias_dram = nc.dram_tensor("mbias_scratch", (B * NT, P), F32, kind="Internal").ap()
    flags_dram = nc.dram_tensor("flags_scratch", (B * NT,), F32, kind="Internal").ap()
    den_dram = nc.dram_tensor("den_scratch", (HG * QH, P, QW), F32, kind="Internal").ap()

    es = ExitStack()
    with es:
        base = (nc.sbuf_base + 31) // 32 * 32
        top = [base]

        def at(name, shape, dt, offset):
            return nc.alloc_sbuf_tensor_at(name, shape, dt, offset=offset).ap()

        def region(nbytes):
            o = top[0]
            top[0] = o + nbytes
            return o

        def own(name, shape, dt=F32):
            n = int(np.prod(shape[1:])) * 4
            return at(name, shape, dt, region((n + 31) // 32 * 32))

        wq_hi, wq_lo = own("wq_hi", [P, KC, D], F32R), own("wq_lo", [P, KC, D], F32R)
        wkT, wvT = own("wkT", [P, KC, D]), own("wvT", [P, KC, D])
        wo_hi, wo_lo = own("wo_hi", [P, KC, D], F32R), own("wo_lo", [P, KC, D], F32R)
        wf_hi, wf_lo = own("wf_hi", [P, KC, D], F32R), own("wf_lo", [P, KC, D], F32R)
        r_q, r_k = region(64 * KB), region(16 * KB)
        qs = at("qs", [P, H, T], F32R, r_q)
        ks = at("ks", [P, HG, 4, GK], F32R, r_k)
        raw = at("raw", [P, 7, KC, D], F32, r_q)
        a1T = at("a1T", [P, KC, D], F32, r_q + 56 * KB)
        wfT = at("wfT", [P, KC, D], F32, r_k)
        m12 = at("m12", [P, KC, D], F32, r_k + 8 * KB)
        vals = own("vals", [P, GT, D])
        r_1 = region(16 * KB)
        attn = at("attn", [P, HG, T], F32, r_1)
        xT_hi, xT_lo = at("xT_hi", [P, KC, QW], F32R, r_1), at("xT_lo", [P, KC, QW], F32R, r_1 + 8 * KB)
        r_2 = region(16 * KB)
        prob = at("prob", [P, 2, 4, QW], F32, r_2)
        x_in, xn_in = prob[:, 0, :, :], prob[:, 1, 0:2, :]
        yT_hi, yT_lo = at("yT_hi", [P, KC, QW], F32R, r_2), at("yT_lo", [P, KC, QW], F32R, r_2 + 8 * KB)
        r_3 = region(8 * KB)
        q_st = at("q_st", [P, 2, 2, QW], F32, r_3)
        k_st = at("k_st", [P, 2, HG, GK], F32, r_3)
        work = at("work", [P, 4, QW], F32, r_3)
        den_sb, den_old, alpha_sb, rden = (work[:, n, :] for n in range(4))
        x_res = at("x_res", [P, 4, D], F32, r_3)
        ctx_sb = own("ctx_sb", [P, GT, D])
        ctxT = own("ctxT", [P, KC, GK])
        y_out = ctxT.rearrange("p a b -> p (a b)").rearrange("p (s n) -> p s n", s=2)
        alpha_x = own("alpha_x", [P, 4, P])
        ident = own("ident", [P, P])
        bv_b, bo_b, fb_b = own("bv_b", [P, D]), own("bo_b", [P, D]), own("fb_b", [P, D])
        m_run = own("m_run", [P, HG, 4 * QT])
        m_new = own("m_new", [P, 4, QT])
        m_tile = own("m_tile", [P, 4, QT])
        m_pair = own("m_pair", [P, 4, 4 * QT])
        m_dif = own("m_dif", [P, 4, QT])
        mT = own("mT", [2 * 4 * QT, P])
        ones32 = own("ones32", [P, 32])
        bq_c, bk_c = own("bq_c", [P, KC]), own("bk_c", [P, KC])
        stat = own("stat", [P, 4, 6])
        mv = own("mv", [P, 4, 2])
        nw = own("nw", [P, 4, 4])
        nf_all, nf_b = own("nf_all", [P, B]), own("nf_b", [P, 1])
        table = own("table", [1, 112], I32)
        assert top[0] <= 229368, top[0]
        ctl = at("ctl", [1, 4096], F32, r_1)
        mask_sb = at("mask_sb", [B * NT, P], I32, r_2)
        meq = at("meq", [B * NT, P], F32, r_2 + 512)
        mbias = at("mbias", [B * NT, P], F32, r_2 + 1024)
        flag = at("flag", [B * NT, 1], F32, r_2 + 1536)

        ps = es.enter_context(nc.psum_tensor("ps", [P, 8, 512], F32))

        def sem(name):
            return es.enter_context(nc.semaphore(name))

        ld_small, ld_w = sem("ld_small"), [sem(f"ld_w{n}") for n in range(7)]
        flags_set, flags_stored, flags_row, stack_rows = sem("flags_set"), sem("flags_stored"), sem("flags_row"), sem("stack_rows")
        mask_ready, table_ready, nf_row, nf_ps = sem("mask_ready"), sem("table_ready"), sem("nf_row"), sem("nf_ps")
        wt_ps, wt_hi, wt_done = sem("wt_ps"), sem("wt_hi"), sem("wt_done")
        m12_ps, m12_done, wf_ps, wf_h, wf_done = (sem(n) for n in ("m12_ps", "m12_done", "wf_ps", "wf_h", "wf_done"))
        x_loaded = [sem(f"x_loaded{n}") for n in range(4)]
        xn_ready, xT_ps, xT_h, xT_l = sem("xn_ready"), sem("xT_ps"), sem("xT_h"), sem("xT_l")
        q_ps, q_h, q_l = sem("q_ps"), sem("q_h"), sem("q_l")
        q_stacked = [sem(f"q_stacked{n}") for n in range(2)]
        ctx_loaded = [sem(f"ctx_loaded{n}") for n in range(GT)]
        ctxT_ps, ctxT_a, ctxT_d = sem("ctxT_ps"), sem("ctxT_a"), sem("ctxT_d")
        k_ps, k_h, k_l, k_stacked = sem("k_ps"), sem("k_h"), sem("k_l"), sem("k_stacked")
        v_ps, v_done = sem("v_ps"), sem("v_done")
        nat_ps, nat_done, m_ready, m_rows = (sem(n) for n in ("nat_ps", "nat_done", "m_ready", "m_rows"))
        s_ps, exp_done, pv_done, o_done = (sem(n) for n in ("s_ps", "exp_done", "pv_done", "o_done"))
        dif_ready, alpha_exp, alpha_ps, alpha_done = (sem(n) for n in ("dif_ready", "alpha_exp", "alpha_ps", "alpha_done"))
        den_loaded, den_used, den_ready, den_saved = (sem(n) for n in ("den_loaded", "den_used", "den_ready", "den_saved"))
        a_h, a_l, oj_ps, x1_done = sem("a_h"), sem("a_l"), sem("oj_ps"), sem("x1_done")
        xr_loaded = [sem(f"xr_loaded{n}") for n in range(4)]
        xb_done, yn_ready, yT_ps, yT_h, yT_l = (sem(n) for n in ("xb_done", "yn_ready", "yT_ps", "yT_h", "yT_l"))
        f_ps, f_b, f_tanh, y_done = (sem(n) for n in ("f_ps", "f_b", "f_tanh", "y_done"))
        y_stored = [sem(f"y_stored{n}") for n in range(2)]
        chain = sem("chain")
        past = {}

        def hold(eng, semaphore, value):
            eng.wait_ge(semaphore, value)
            eng.sem_inc(past[eng], 1)

        PIECES = 2 * QT
        NATS = PIECES + 1
        SHARE = (6, 6, 4, 0)

        def groups(eng, b):
            first = eng.value_load(table[0:1, DS(b, 1)], min_val=0, max_val=B * NT // GT)
            count = eng.value_load(table[0:1, DS(b + 8, 1)], min_val=1, max_val=NT // GT)
            return first, count

        def later(eng, b, i):
            before = eng.value_load(table[0:1, DS(b + 12, 1)], min_val=0, max_val=24)
            return eng.value_load(table[0:1, DS(before + i + 80, 1)], min_val=0, max_val=31)

        def unfinished(eng, b, i):
            return eng.value_load(table[0:1, DS(b + 12, 1)], min_val=0, max_val=24) + i

        def end_group(eng, b):
            return eng.value_load(table[0:1, DS(b + 1, 1)], min_val=1, max_val=B * NT // GT)

        block = es.enter_context(nc.Block())

        @block.sync
        def _(sp):
            past[sp] = sem("sp_past")
            sp.dma_start(mask_sb[:, :], mask_rows).then_inc(mask_ready, 16)
            sp.dma_start(ident[:, :], ident_in).then_inc(ld_small, 16)
            sp.dma_start(ctl[0:1, 0:NROW], rows_in).then_inc(ld_small, 16)
            for n, w in enumerate((wq, wk, wv, wa1, wa2, wf, wo)):
                sp.dma_start(raw[:, n, :, :], w.rearrange("(r p) c -> p r c", p=P)).then_inc(ld_w[n], 16)
                if n == 0:
                    with nc.allow_non_contiguous_dma(reason="512 words each, once"):
                        sp.dma_start(bq_c[:, :], bq.rearrange("(m p) -> p m", p=P)).then_inc(ld_small, 16)
                        sp.dma_start(bk_c[:, :], bk.rearrange("(m p) -> p m", p=P)).then_inc(ld_small, 16)
                    for dst, src in ((bv_b, bv), (bo_b, bo), (fb_b, fb)):
                        sp.dma_start(dst[:, :], src.partition_broadcast(P)).then_inc(ld_small, 16)
            sp.wait_ge(flags_set, 1)
            sp.dma_start(mbias_dram, mbias[:, :]).then_inc(flags_stored, 16)
            sp.dma_start(flags_dram.rearrange("(p a) -> p a", a=1), flag[:, :]).then_inc(flags_stored, 16)
            sp.wait_ge(flags_stored, 32)
            sp.dma_start(ctl[0:1, 192:256], flags_dram.rearrange("(a p) -> a p", a=1)).then_inc(flags_row, 16)
            sp.wait_ge(table_ready, 1)
            sp.wait_ge(stack_rows, 2)
            with sp.Fori(0, B) as b:
                for t in range(QT):
                    if t == 0:
                        hold(sp, f_ps, b * QT)
                    if t >= 4:
                        hold(sp, xn_ready, b * QT + t - 3)
                    sp.dma_start(x_in[:, t % 4, :], x_rows[DS(b * T + t * P, P), :]).then_inc(x_loaded[t % 4], 16)
                for n in range(QH * HG):
                    qh, m = divmod(n, HG)
                    sp.wait_ge(q_l, b * (QH * HG) + n + 1)
                    for g in range(4):
                        rows = slice(32 * g, 32 * g + 32)
                        cols = slice(qh * QW, qh * QW + QW)
                        for r0, part in ((0, 0), (32, 1), (64, 0)):
                            sp.dma_start(qs[r0:r0 + 32, 4 * m + g, cols].bitcast(F32),
                                         q_st[rows, n % 2, part, :]).then_inc(q_stacked[n % 2], 16)
                first, count = groups(sp, b)
                with sp.Fori(0, count) as i:
                    k = first + i
                    tiles = [sp.value_load(table[0:1, DS(16 + b * NT + i * GT + j, 1)], min_val=0, max_val=B * NT - 1)
                             for j in range(GT)]
                    rows = [sp.snap(tiles[j] * P) for j in range(GT)]
                    hold(sp, ctxT_ps, k)
                    for j in range(GT):
                        sp.dma_start(ctx_sb[:, j, :], ctx_rows[DS(rows[j], P), :]).then_inc(ctx_loaded[j], 16)
                    hold(sp, k_l, 2 * k + 2)
                    for j in range(GT):
                        sp.dma_start(ks[96:97, :, :, j * P:(j + 1) * P].bitcast(F32).rearrange("p a b k -> p (a b) k"),
                                     mbias_dram[DS(tiles[j], 1), :].unsqueeze(1).to_broadcast([1, H, P])
                                     ).then_inc(k_stacked, 16)
                    for g in range(4):
                        rows = slice(32 * g, 32 * g + 32)
                        for r0, part in ((0, 0), (32, 0), (64, 1)):
                            sp.dma_start(ks[r0:r0 + 32, :, g, :].bitcast(F32), k_st[rows, part, :, :]).then_inc(k_stacked, 16)
                    for hg in range(HG):
                        sp.wait_ge(nat_done, (k * HG + hg + 1) * NATS)
                        for part in range(2):
                            sp.dma_start(qs[97 + part:98 + part, 4 * hg:4 * hg + 4, :].bitcast(F32).rearrange("p a (b c) -> p (a b) c", c=P),
                                         mT[32 * part:32 * part + 32, :]).then_inc(m_rows, 16)
                last = end_group(sp, b)
                hold(sp, o_done, last * (HG * QH))
                for t in range(4):
                    sp.dma_start(x_res[:, t, :], x_rows[DS(b * T + t * P, P), :]).then_inc(xr_loaded[t], 16)
                for t in range(QT):
                    hold(sp, y_done, b * QT + t + 1)
                    sp.dma_start(out_rows[DS(b * T + t * P, P), :], y_out[:, t % 2, :]).then_inc(y_stored[t % 2], 16)
                    if t < 4:
                        sp.dma_start(x_res[:, t, :], x_rows[DS(b * T + (t + 4) * P, P), :]).then_inc(xr_loaded[t], 16)
            for n in range(2):
                sp.wait_ge(y_stored[n], B * QT // 2 * 16)

        @block.tensor
        def _(pe):
            past[pe] = sem("pe_past")
            pe.wait_ge(ld_small, 16 * 7)
            bank = 0
            for n in (0, 1, 2, 3, 5, 6):
                pe.wait_ge(ld_w[n], 16)
                for kc in range(KC):
                    if bank >= 4:
                        pe.wait_ge(wt_done, bank - 3)
                    for r in range(KC):
                        last = nc.tensor.transpose(ps[:, bank % 4, r * P:(r + 1) * P],
                                                   raw[:, n, r, kc * P:(kc + 1) * P], ident[:, :])
                    last.then_inc(wt_ps, 1)
                    bank += 1
            pe.wait_ge(wt_done, bank)
            pe.wait_ge(ld_w[4], 16)
            for m in range(KC):
                for kc in range(KC):
                    last = nc.tensor.matmul(ps[:, 4 + m, :], a1T[:, kc, m * P:(m + 1) * P], raw[:, 4, kc, :],
                                            start=kc == 0, stop=kc == KC - 1)
                last.then_inc(m12_ps, 1)
            pe.wait_ge(m12_done, KC)
            for m in range(KC):
                for kc in range(KC):
                    last = nc.tensor.matmul(ps[:, 4 + m, :], wfT[:, kc, m * P:(m + 1) * P], m12[:, kc, :],
                                            start=kc == 0, stop=kc == KC - 1)
                last.then_inc(wf_ps, 1)
            pe.wait_ge(nf_row, 1)
            pe.wait_ge(stack_rows, 2)
            pe.wait_ge(wf_done, 1)
            nc.tensor.matmul(ps[:, 4, 0:B], ctl[0:1, 3840:3968], ctl[0:1, 3968:3968 + B], start=True, stop=True).then_inc(nf_ps, 1)
            pe.wait_ge(table_ready, 1)

            with pe.Fori(0, B) as b:
                for qh in range(QH):
                    for i in range(4):
                        t = 4 * qh + i
                        pe.wait_ge(xn_ready, b * QT + t + 1)
                        if qh:
                            pe.wait_ge(xT_l, b * QT + t - 3)
                        for kc in range(KC):
                            last = nc.tensor.transpose(ps[:, i, kc * P:(kc + 1) * P], xn_in[:, t % 2, kc * P:(kc + 1) * P], ident[:, :])
                        last.then_inc(xT_ps, 1)
                    pe.wait_ge(xT_l, b * QT + 4 * qh + 4)
                    for m in range(HG):
                        n = qh * HG + m
                        if n >= 2:
                            pe.wait_ge(q_l, b * (QH * HG) + n - 1)
                        cols = slice(m * P, (m + 1) * P)
                        step = 0
                        for kc in range(KC):
                            for w, a in ((wq_hi, xT_hi), (wq_hi, xT_lo), (wq_lo, xT_hi)):
                                last = nc.tensor.matmul(ps[:, 4 + n % 2, :], w[:, kc, cols], a[:, kc, :],
                                                        start=step == 0, stop=step == 3 * KC - 1)
                                step += 1
                        last.then_inc(q_ps, 1)

                first, count = groups(pe, b)
                with pe.Fori(0, count) as i:
                    k = first + i

                    def nat(hg, p):
                        n = hg * NATS + p
                        pe.wait_ge(nat_done, k * (HG * NATS) + n - 1) if n >= 1 else pe.wait_ge(v_done, k * GT + GT)
                        qt, pair = divmod(p, 2)
                        for s in range(2):
                            g = 2 * pair + s
                            last = nc.tensor.matmul(ps[:, 4 + n % 2, s * GK:(s + 1) * GK],
                                                    qs[0:97, 4 * hg + g, qt * P:(qt + 1) * P],
                                                    ks[0:97, hg, g, :], start=True, stop=True)
                        last.then_inc(nat_ps, 1)

                    def maxT(hg):
                        n = hg * NATS + PIECES
                        pe.wait_ge(m_ready, k * HG + hg + 1)
                        nc.tensor.transpose(ps[:, 4 + n % 2, 0:P],
                                            m_pair[:, :, :].rearrange("p a b -> p (a b)"), ident[:, :]).then_inc(nat_ps, 1)

                    def scores(hg, u):
                        qh, j = divmod(u, GT)
                        if u == 0:
                            pe.wait_ge(m_rows, (k * HG + hg + 1) * 32)
                        for pair in range(2):
                            e = (hg * 4 + u) * 2 + pair
                            pe.wait_ge(exp_done, k * 32 + e - 1) if e >= 2 else pe.wait_ge(exp_done, k * 32)
                            for s in range(2):
                                g = 2 * pair + s
                                last = nc.tensor.matmul(ps[:, 2 * pair + s, :], ks[0:99, hg, g, j * P:(j + 1) * P],
                                                        qs[0:99, 4 * hg + g, qh * QW:(qh + 1) * QW],
                                                        start=True, stop=True)
                            last.then_inc(s_ps, 1)

                    def weigh(hg, u):
                        qh, j = divmod(u, GT)
                        w = hg * QH + qh
                        if j == 0:
                            pe.wait_ge(o_done, k * (HG * QH) + w)
                            with pe.If(i > 0):
                                late = later(pe, b, i)
                                pe.wait_ge(alpha_exp, late * (HG * QH) + w + 1)
                                for c in range(4):
                                    last = nc.tensor.transpose(ps[:, 6, c * P:(c + 1) * P], alpha_x[:, c, :], ident[:, :])
                                last.then_inc(alpha_ps, 1)
                                hold(pe, alpha_done, late * (HG * QH) + w + 1)
                        pe.wait_ge(exp_done, k * 32 + (hg * 4 + u) * 2 + 2)
                        for g in range(4):
                            h = 4 * hg + g
                            nc.tensor.matmul(ps[32 * g:32 * g + 32, 6, :], vals[:, j, h * DK:(h + 1) * DK],
                                             prob[:, u % 2, g, :], start=j == 0, stop=j == GT - 1)
                        for g in range(4):
                            last = nc.tensor.matmul(ps[32 * g:32 * g + 32, 7, :], ones32[:, :],
                                                    prob[:, u % 2, g, :], start=j == 0, stop=j == GT - 1)
                        last.then_inc(pv_done, 1)

                    pe.wait_ge(o_done, k * (HG * QH))
                    for n in range(2):
                        pe.wait_ge(y_stored[n], b * 64)
                    for j in range(GT):
                        pe.wait_ge(ctx_loaded[j], k * 16 + 16)
                        for kc in range(KC):
                            last = nc.tensor.transpose(ps[:, j, kc * P:(kc + 1) * P], ctx_sb[:, j, kc * P:(kc + 1) * P], ident[:, :])
                    last.then_inc(ctxT_ps, 1)
                    pe.wait_ge(ctxT_a, k + 1)
                    pe.wait_ge(ctxT_d, k + 1)
                    for m in range(HG):
                        for kc in range(KC):
                            last = nc.tensor.matmul(ps[:, 2 + m // 2, (m % 2) * GK:(m % 2 + 1) * GK],
                                                    wkT[:, kc, m * P:(m + 1) * P], ctxT[:, kc, :],
                                                    start=kc == 0, stop=kc == KC - 1)
                        if m % 2:
                            last.then_inc(k_ps, 1)
                    pe.wait_ge(q_l, b * 8 + 8)
                    for j in range(GT):
                        for kc in range(KC):
                            last = nc.tensor.matmul(ps[:, 4 + j, :], ctxT[:, kc, j * P:(j + 1) * P], wvT[:, kc, :],
                                                    start=kc == 0, stop=kc == KC - 1)
                        last.then_inc(v_ps, 1)
                    for n in range(2):
                        pe.wait_ge(q_stacked[n], (b + 1) * (4 * 12 * 16))
                    pe.wait_ge(k_stacked, (k + 1) * (14 * 16))
                    for p in range(PIECES):
                        nat(0, p)
                    maxT(0)
                    for hg in range(HG):
                        p = 0
                        for u in range(4):
                            if u == 0 and hg:
                                weigh(hg - 1, 3)
                            scores(hg, u)
                            if u == 3 and hg + 1 < HG:
                                maxT(hg + 1)
                            if u:
                                weigh(hg, u - 1)
                            if hg + 1 < HG:
                                for _ in range(SHARE[u]):
                                    nat(hg + 1, p)
                                    p += 1
                    weigh(HG - 1, 3)

                for qh in range(QH):
                    pe.wait_ge(a_l, b * QH + qh + 1)
                    for i in range(4):
                        t = 4 * qh + i
                        if i >= 2:
                            pe.wait_ge(x1_done, b * QT + t - 1)
                        rows = slice(i * P, (i + 1) * P)
                        step = 0
                        for kc in range(KC):
                            for a, w in ((yT_hi, wo_hi), (yT_hi, wo_lo), (yT_lo, wo_hi)):
                                last = nc.tensor.matmul(ps[:, i % 2, :], a[:, kc, rows], w[:, kc, :],
                                                        start=step == 0, stop=step == 3 * KC - 1)
                                step += 1
                        last.then_inc(oj_ps, 1)
                    for i in range(4):
                        t = 4 * qh + i
                        pe.wait_ge(yn_ready, b * QT + t + 1)
                        if i >= 2:
                            pe.wait_ge(yT_l, b * QT + t - 1)
                        for kc in range(KC):
                            last = nc.tensor.transpose(ps[:, 2 + i % 2, kc * P:(kc + 1) * P], vals[:, t % 2, kc * P:(kc + 1) * P], ident[:, :])
                        last.then_inc(yT_ps, 1)
                    for i in range(4):
                        t = 4 * qh + i
                        pe.wait_ge(yT_l, b * QT + t + 1)
                        if i >= 2:
                            pe.wait_ge(f_b, b * QT + t - 1)
                        rows = slice(i * P, (i + 1) * P)
                        step = 0
                        for kc in range(KC):
                            for a, w in ((yT_hi, wf_hi), (yT_hi, wf_lo), (yT_lo, wf_hi)):
                                last = nc.tensor.matmul(ps[:, 4 + i % 2, :], a[:, kc, rows], w[:, kc, :],
                                                        start=step == 0, stop=step == 3 * KC - 1)
                                step += 1
                        last.then_inc(f_ps, 1)

        @block.scalar
        def _(act):
            bank = 0
            for n in (0, 1, 2, 3, 5, 6):
                for kc in range(KC):
                    if n in (0, 6):
                        act.wait_ge(wt_ps, bank + 1)
                        nc.scalar.activation((wq_hi if n == 0 else wo_hi)[:, kc, :], ps[:, bank % 4, :], ACT.Copy).then_inc(wt_hi, 1)
                    bank += 1
            for m in range(KC):
                act.wait_ge(m12_ps, m + 1)
                nc.scalar.activation(m12[:, m, :], ps[:, 4 + m, :], ACT.Copy).then_inc(m12_done, 1)
            for m in range(KC):
                act.wait_ge(wf_ps, m + 1)
                nc.scalar.activation(wf_hi[:, m, :], ps[:, 4 + m, :], ACT.Copy).then_inc(wf_h, 1)
            act.wait_ge(table_ready, 1)
            act.wait_ge(ld_small, 16 * 7)

            with act.Fori(0, B) as b:
                for qh in range(QH):
                    for i in range(4):
                        t = 4 * qh + i
                        act.wait_ge(xT_ps, b * QT + t + 1)
                        if qh and i == 0:
                            act.wait_ge(q_ps, b * 8 + 4)
                        nc.scalar.activation(xT_hi[:, :, i * P:(i + 1) * P], ps[:, i, :].rearrange("p (a c) -> p a c", c=P),
                                             ACT.Copy).then_inc(xT_h, 1)
                    for m in range(HG):
                        n = qh * HG + m
                        act.wait_ge(q_ps, b * 8 + n + 1)
                        if n == 0:
                            act.wait_ge(y_done, b * QT)
                        if n >= 2:
                            act.wait_ge(q_stacked[n % 2], (b * 4 + n // 2) * (12 * 16))
                        nc.scalar.activation(q_st[:, n % 2, 0, :].bitcast(F32R), ps[:, 4 + n % 2, :], ACT.Identity,
                                             bias=bq_c[:, m:m + 1]).then_inc(q_h, 1)
                first, count = groups(act, b)
                with act.Fori(0, count) as i:
                    k = first + i
                    act.wait_ge(ctxT_ps, k + 1)
                    nc.scalar.activation(ctxT[:, :, 0:P], ps[:, 0, :].rearrange("p (a c) -> p a c", c=P), ACT.Copy).then_inc(ctxT_a, 1)
                    for n in range(2):
                        act.wait_ge(q_stacked[n], (b + 1) * (4 * 12 * 16))
                    for m in range(HG):
                        if m % 2 == 0:
                            act.wait_ge(k_ps, k * 2 + m // 2 + 1)
                        nc.scalar.activation(k_st[:, 0, m, :].bitcast(F32R), ps[:, 2 + m // 2, (m % 2) * GK:(m % 2 + 1) * GK],
                                             ACT.Identity, bias=bk_c[:, m:m + 1]).then_inc(k_h, 1)
                    for hg in range(HG):
                        for u in range(4):
                            if u % 2 == 0:
                                qh = u // 2
                                with act.If(i > 0):
                                    late = later(act, b, i)
                                    act.wait_ge(dif_ready, late * HG + hg + 1)
                                    act.wait_ge(alpha_ps, late * (HG * QH) + hg * QH + qh)
                                    for c in range(4):
                                        last = nc.scalar.activation(
                                            alpha_x[:, c, :].rearrange("p (g r) -> p g r", r=32),
                                            m_dif[:, :, 4 * qh + c:4 * qh + c + 1].to_broadcast([P, 4, 32]), ACT.Exp, scale=SCALE)
                                    last.then_inc(alpha_exp, 1)
                            for pair in range(2):
                                e = (hg * 4 + u) * 2 + pair
                                act.wait_ge(s_ps, k * 32 + e + 1)
                                act.wait_ge(pv_done, k * 16 + hg * 4 + u - 1) if hg * 4 + u >= 1 else act.wait_ge(pv_done, k * 16)
                                nc.scalar.activation(prob[:, u % 2, 2 * pair:2 * pair + 2, :], ps[:, 2 * pair:2 * pair + 2, :],
                                                     ACT.Exp, scale=SCALE).then_inc(exp_done, 1)
                last_group = end_group(act, b)
                for qh in range(QH):
                    act.wait_ge(o_done, last_group * 8)
                    if qh:
                        act.wait_ge(f_ps, b * QT + 4)
                    else:
                        act.wait_ge(pv_done, last_group * 16)
                    nc.scalar.activation(yT_hi[:, :, :], attn[:, :, qh * QW:(qh + 1) * QW], ACT.Copy, scale=nf_b[:, 0:1]).then_inc(a_h, 1)
                    for i in range(4):
                        t = 4 * qh + i
                        act.wait_ge(yT_ps, b * QT + t + 1)
                        nc.scalar.activation(yT_hi[:, :, i * P:(i + 1) * P], ps[:, 2 + i % 2, :].rearrange("p (a c) -> p a c", c=P),
                                             ACT.Copy).then_inc(yT_h, 1)
                    for i in range(4):
                        t = 4 * qh + i
                        act.wait_ge(f_b, b * QT + t + 1)
                        nc.scalar.activation(y_out[:, t % 2, :], y_out[:, t % 2, :], ACT.Tanh).then_inc(f_tanh, 1)

        @block.gpsimd
        def _(pool):
            past[pool] = sem("pool_past")
            pool.wait_ge(wf_ps, KC)
            nc.gpsimd.memset(qs[96:P, :, :].bitcast(F32), 1.0).then_inc(stack_rows, 1)
            pool.wait_ge(stack_rows, 1)
            nc.gpsimd.memset(ks[96:P, :, :, :].bitcast(F32), -1.0).then_inc(stack_rows, 1)
            pool.wait_ge(table_ready, 1)
            with pool.Fori(0, B) as b:
                first, count = groups(pool, b)
                with pool.Fori(0, count) as i:
                    k = first + i
                    for w in range(HG * QH):
                        with pool.If(i > 0):
                            late = later(pool, b, i)
                            hold(pool, dif_ready, late * HG + w // QH + 1)
                            hold(pool, den_used, late * (HG * QH) + w)
                            pool.dma_start(den_old, den_dram[w, :, :]).then_inc(den_loaded, 16)
                        with pool.If(i + 1 < count):
                            unfin = unfinished(pool, b, i)
                            hold(pool, den_ready, unfin * (HG * QH) + w + 1)
                            pool.dma_start(den_dram[w, :, :], den_sb).then_inc(den_saved, 16)
                            hold(pool, den_saved, (unfin * (HG * QH) + w + 1) * 16)
                for t in range(QT):
                    pool.wait_ge(xr_loaded[t % 4], (b * 2 + t // 4 + 1) * 16)
                    nc.gpsimd.tensor_tensor(x_res[:, t % 4, :], x_res[:, t % 4, :], bo_b[:, :], ALU.add).then_inc(xb_done, 1)
                    if t % 4 == 3:
                        for i in range(4):
                            tt = t - 3 + i
                            pool.wait_ge(f_tanh, b * QT + tt + 1)
                            nc.gpsimd.tensor_tensor(y_out[:, tt % 2, :], y_out[:, tt % 2, :], x_res[:, tt % 4, :], ALU.add).then_inc(y_done, 1)

        @block.vector
        def _(dve):
            past[dve] = sem("dve_past")
            links = [0]

            def link(ins):
                links[0] += 1
                ins.then_inc(chain, 1)
                dve.wait_ge(chain, links[0])

            def cut():
                links[0] = 0
                dve.sem_clear(chain)

            V = nc.vector

            dve.wait_ge(mask_ready, 16)
            link(V.tensor_scalar(meq[:, :], mask_sb[:, :], 0.0, None, ALU.is_equal))
            V.tensor_scalar(mbias[:, :], meq[:, :], MASKED, None, ALU.mult)
            link(V.tensor_reduce(flag[:, :], meq[:, :], AX, ALU.min))
            V.memset(ones32[:, :], 1.0)
            V.memset(ctl[0:1, 3840:3968], 1.0).then_inc(flags_set, 1)

            bank = 0
            def weights(ns):
                nonlocal bank
                for n in ns:
                    for kc in range(KC):
                        dve.wait_ge(wt_ps, bank + 1)
                        src = ps[:, bank % 4, :]
                        if n in (0, 6):
                            hi, lo = (wq_hi, wq_lo) if n == 0 else (wo_hi, wo_lo)
                            dve.wait_ge(wt_hi, (0 if n == 0 else 4) + kc + 1)
                            V.tensor_tensor(lo[:, kc, :], src, hi[:, kc, :].bitcast(F32), ALU.subtract).then_inc(wt_done, 1)
                        else:
                            dst = {1: wkT, 2: wvT, 3: a1T, 5: wfT}[n]
                            V.tensor_copy(dst[:, kc, :], src).then_inc(wt_done, 1)
                        bank += 1

            weights((0, 1, 2))

            dve.wait_ge(flags_row, 16)
            dve.wait_ge(ld_small, 16 * 7)
            tno, b16 = ctl[0:1, 0:64], ctl[0:1, 64:128]
            ev, low = ctl[0:1, 128:136], ctl[0:1, 136:156]
            e, key, rank = ctl[0:1, 192:256], ctl[0:1, 256:320], ctl[0:1, 320:384]
            perm, n_act, grp = ctl[0:1, 384:448], ctl[0:1, 448:452], ctl[0:1, 456:460]
            gt8, cum5, acc = ctl[0:1, 464:496], ctl[0:1, 496:516], ctl[0:1, 520:525]
            val, act_t = ctl[0:1, 528:532], ctl[0:1, 536:600]
            cmp4 = ctl[0:1, 1024:2048].rearrange("p (b t u) -> p b t u", b=B, t=NT)
            link(V.scalar_tensor_tensor(key, e, float(NT), tno, ALU.mult, ALU.add))
            k3 = key.rearrange("p (b t) -> p b t", b=B)
            link(V.tensor_tensor(cmp4, k3.unsqueeze(2).to_broadcast([1, B, NT, NT]),
                                 k3.unsqueeze(3).to_broadcast([1, B, NT, NT]), ALU.is_lt))
            link(V.tensor_reduce(rank.rearrange("p (b t) -> p b t", b=B), cmp4, AX, ALU.add))
            r3 = rank.rearrange("p (b t) -> p b t", b=B)
            t3 = tno.rearrange("p (b t) -> p b t", b=B)
            link(V.tensor_tensor(cmp4, r3.unsqueeze(2).to_broadcast([1, B, NT, NT]),
                                 t3.unsqueeze(3).to_broadcast([1, B, NT, NT]), ALU.is_equal))
            link(V.tensor_tensor(cmp4, cmp4, t3.unsqueeze(2).to_broadcast([1, B, NT, NT]), ALU.mult))
            link(V.tensor_reduce(perm.rearrange("p (b t) -> p b t", b=B), cmp4, AX, ALU.add))
            V.tensor_tensor(table[0:1, 16:80], perm, b16, ALU.add)
            link(V.tensor_scalar(act_t, e, -1.0, 1.0, ALU.mult, ALU.add))
            link(V.tensor_reduce(n_act, act_t.rearrange("p (b t) -> p b t", b=B), AX, ALU.add))
            g3 = gt8.rearrange("p (b i) -> p b i", b=B)
            link(V.tensor_tensor(g3, n_act.unsqueeze(2).to_broadcast([1, B, 8]), ev.unsqueeze(1).to_broadcast([1, B, 8]), ALU.is_gt))
            link(V.tensor_reduce(grp, g3, AX, ALU.add))
            link(V.tensor_scalar(grp, grp, 1.0, None, ALU.max))
            V.tensor_copy(table[0:1, 8:12], grp)
            c3 = cum5.rearrange("p (j b) -> p j b", b=B)
            link(V.tensor_tensor(c3, grp.unsqueeze(1).to_broadcast([1, B + 1, B]), low.rearrange("p (j b) -> p j b", b=B), ALU.mult))
            link(V.tensor_reduce(acc, c3, AX, ALU.add))
            V.tensor_copy(table[0:1, 80:112], ctl[0:1, 160:192])
            V.tensor_tensor(table[0:1, 12:16], acc[:, 0:4], ctl[0:1, 156:160], ALU.subtract)
            link(V.tensor_copy(table[0:1, 0:5], acc))
            link(V.tensor_scalar(val, n_act, 1.0, None, ALU.min))
            link(V.reciprocal(ctl[0:1, 3980:3984], val))
            V.tensor_tensor(ctl[0:1, 3968:3972], val, ctl[0:1, 3980:3984], ALU.mult).then_inc(nf_row, 1)

            weights((3, 5, 6))
            for m in range(KC):
                dve.wait_ge(wf_h, m + 1)
                V.tensor_tensor(wf_lo[:, m, :], ps[:, 4 + m, :], wf_hi[:, m, :].bitcast(F32), ALU.subtract).then_inc(wf_done, 1)
            dve.wait_ge(nf_ps, 1)
            link(V.tensor_copy(nf_all[:, :], ps[:, 4, 0:B]))
            cut()
            V.memset(m_pair[:, :, :], 0.0).then_inc(table_ready, 1)

            def newton():
                a, y, t_, n_ = (nw[:, q, :] for q in range(4))
                link(V.tensor_scalar(a, mv[:, :, 1], EPS, None, ALU.add))
                link(V.tensor_scalar(n_.bitcast(I32), a.bitcast(I32), 1, None, ALU.arith_shift_right))
                link(V.tensor_scalar(y.bitcast(I32), n_.bitcast(I32), -1.0, float(0x5F3759DF), ALU.mult, ALU.add))
                for _ in range(4):
                    link(V.scalar_tensor_tensor(t_, y, -0.5, y, ALU.mult, ALU.mult))
                    link(V.tensor_tensor(t_, t_, a, ALU.mult))
                    link(V.scalar_tensor_tensor(y, t_, 1.5, y, ALU.add, ALU.mult))

            with dve.Fori(0, B) as b:
                V.memset(m_run[:, :, :], LOWEST)
                link(V.tensor_copy(nf_b[:, :], nf_all[:, DS(b, 1)]))
                for qh in range(QH):
                    for i in range(4):
                        dve.wait_ge(x_loaded[i], (b * 2 + qh + 1) * 16)
                        last = V.bn_stats(stat[:, i, :], x_in[:, i, :])
                    link(last)
                    for i in range(4):
                        last = V.bn_aggr(mv[:, i, :], stat[:, i, :])
                    link(last)
                    newton()
                    for i in range(4):
                        t = 4 * qh + i
                        if t >= 2:
                            dve.wait_ge(xT_ps, b * QT + t - 1)
                        V.tensor_scalar(xn_in[:, t % 2, :], x_in[:, i, :], mv[:, i, 0:1], nw[:, 1, i:i + 1],
                                        ALU.subtract, ALU.mult).then_inc(xn_ready, 1)
                    for i in range(4):
                        t = 4 * qh + i
                        dve.wait_ge(xT_h, b * QT + t + 1)
                        sl = (slice(None), slice(None), slice(i * P, (i + 1) * P))
                        V.tensor_tensor(xT_lo[sl], ps[:, i, :].rearrange("p (a c) -> p a c", c=P), xT_hi[sl].bitcast(F32),
                                        ALU.subtract).then_inc(xT_l, 1)
                    for m in range(HG):
                        n = qh * HG + m
                        dve.wait_ge(q_h, b * 8 + n + 1)
                        V.scalar_tensor_tensor(q_st[:, n % 2, 1, :].bitcast(F32R), ps[:, 4 + n % 2, :], bq_c[:, m:m + 1],
                                               q_st[:, n % 2, 0, :], ALU.add, ALU.subtract).then_inc(q_l, 1)
                    cut()
                first, count = groups(dve, b)
                with dve.Fori(0, count) as i:
                    k = first + i

                    def reduce(hg, p):
                        n = hg * NATS + p
                        dve.wait_ge(nat_ps, k * (HG * NATS) + n + 1)
                        qt, pair = divmod(p, 2)
                        V.tensor_reduce(m_tile[:, 2 * pair:2 * pair + 2, qt:qt + 1].rearrange("p a b -> p (a b)"),
                                        ps[:, 4 + n % 2, :].rearrange("p (a c) -> p a c", c=GK), AX, ALU.max).then_inc(nat_done, 1)

                    def maxima(hg):
                        dve.wait_ge(nat_done, k * (HG * NATS) + hg * NATS + PIECES)
                        run = m_run[:, hg, :].rearrange("p (a b) -> p a b", b=QT)
                        link(V.tensor_tensor(m_new[:, :, :], m_tile[:, :, :], run, ALU.max))
                        with dve.If(i > 0):
                            late = later(dve, b, i)
                            dve.wait_ge(alpha_exp, late * (HG * QH) + hg * QH)
                            V.tensor_tensor(m_dif[:, :, :], run, m_new[:, :, :], ALU.subtract).then_inc(dif_ready, 1)
                            hold(dve, dif_ready, late * HG + hg + 1)
                        V.tensor_copy(run, m_new[:, :, :])
                        hi, lo = m_pair[:, 0, :], m_pair[:, 1, :]
                        new = m_new[:, :, :].rearrange("p a b -> p (a b)")
                        link(V.tensor_copy(hi.bitcast(F32R), new))
                        V.tensor_tensor(lo, new, hi, ALU.subtract).then_inc(m_ready, 1)
                        cut()

                    def rows(hg):
                        n = hg * NATS + PIECES
                        dve.wait_ge(nat_ps, k * (HG * NATS) + n + 1)
                        dve.wait_ge(m_rows, (k * HG + hg) * 32)
                        V.tensor_copy(mT[:, :], ps[0:64, 4 + n % 2, 0:P]).then_inc(nat_done, 1)

                    def unit_out(hg, qh):
                        w = hg * QH + qh
                        dst = attn[:, hg, qh * QW:(qh + 1) * QW]
                        dve.wait_ge(pv_done, k * 16 + 2 * w + 2)
                        link(V.tensor_copy(den_sb, ps[:, 7, :]))
                        cut()
                        with dve.If(i > 0):
                            late = later(dve, b, i)
                            dve.wait_ge(den_loaded, (late * (HG * QH) + w + 1) * 16)
                            V.tensor_tensor(rden, den_old, alpha_sb, ALU.mult).then_inc(chain, 1)
                            dve.wait_ge(chain, 1)
                            V.tensor_tensor(den_sb, den_sb, rden, ALU.add)
                            V.tensor_tensor(dst, dst, rden, ALU.mult).then_inc(chain, 1)
                            dve.wait_ge(chain, 2)
                            V.tensor_tensor(dst, ps[:, 6, :], dst, ALU.add).then_inc(chain, 1)
                            dve.wait_ge(chain, 3)
                            V.reciprocal(rden, den_sb).then_inc(chain, 1)
                            dve.wait_ge(chain, 4)
                            V.tensor_tensor(dst, dst, rden, ALU.mult).then_inc(chain, 1)
                            dve.wait_ge(chain, 5)
                            dve.sem_clear(chain)
                            dve.sem_inc(den_used, 1)
                            dve.sem_inc(o_done, 1)
                        with dve.If(i < 1):
                            V.reciprocal(rden, den_sb).then_inc(chain, 1)
                            dve.wait_ge(chain, 1)
                            dve.sem_clear(chain)
                            V.tensor_tensor(dst, ps[:, 6, :], rden, ALU.mult).then_inc(o_done, 1)
                        with dve.If(i + 1 < count):
                            unfin = unfinished(dve, b, i)
                            dve.sem_inc(den_ready, 1)
                            hold(dve, den_saved, (unfin * (HG * QH) + w + 1) * 16)

                    def factors(hg, qh):
                        w = hg * QH + qh
                        with dve.If(i > 0):
                            late = later(dve, b, i)
                            dve.wait_ge(alpha_ps, late * (HG * QH) + w + 1)
                            V.tensor_copy(alpha_sb, ps[:, 6, :]).then_inc(alpha_done, 1)

                    dve.wait_ge(ctxT_ps, k + 1)
                    V.tensor_copy(ctxT[:, :, P:2 * P], ps[:, 1, :].rearrange("p (a c) -> p a c", c=P)).then_inc(ctxT_d, 1)
                    for m in range(HG):
                        if m % 2 == 0:
                            dve.wait_ge(k_h, k * HG + m + 2)
                        ins = V.scalar_tensor_tensor(k_st[:, 1, m, :].bitcast(F32R), ps[:, 2 + m // 2, (m % 2) * GK:(m % 2 + 1) * GK],
                                                     bk_c[:, m:m + 1], k_st[:, 0, m, :], ALU.add, ALU.subtract)
                        if m % 2:
                            ins.then_inc(k_l, 1)
                    for j in range(GT):
                        dve.wait_ge(v_ps, k * GT + j + 1)
                        V.tensor_tensor(vals[:, j, :], ps[:, 4 + j, :], bv_b[:, :], ALU.add).then_inc(v_done, 1)
                    for p in range(PIECES):
                        reduce(0, p)
                    maxima(0)
                    rows(0)
                    for hg in range(HG):
                        p = 0
                        for u in range(4):
                            if u == 0 and hg:
                                unit_out(hg - 1, 1)
                            if u == 3 and hg + 1 < HG:
                                rows(hg + 1)
                            if u == 1:
                                factors(hg, 0)
                            if u == 2:
                                unit_out(hg, 0)
                            if u == 3:
                                factors(hg, 1)
                            if hg + 1 < HG:
                                for _ in range(SHARE[u]):
                                    reduce(hg + 1, p)
                                    p += 1
                                if u == 2:
                                    maxima(hg + 1)
                    unit_out(HG - 1, 1)

                for qh in range(QH):
                    dve.wait_ge(a_h, b * QH + qh + 1)
                    for kc in range(KC):
                        last = V.scalar_tensor_tensor(yT_lo[:, kc, :], attn[:, kc, qh * QW:(qh + 1) * QW], nf_b[:, 0:1],
                                                      yT_hi[:, kc, :].bitcast(F32), ALU.mult, ALU.subtract)
                    last.then_inc(a_l, 1)
                    for i in range(4):
                        t = 4 * qh + i
                        dve.wait_ge(oj_ps, b * QT + t + 1)
                        dve.wait_ge(xb_done, b * QT + t + 1)
                        V.tensor_tensor(x_res[:, i, :], ps[:, i % 2, :], x_res[:, i, :], ALU.add).then_inc(x1_done, 1)
                        dve.wait_ge(x1_done, b * QT + t + 1)
                        last = V.bn_stats(stat[:, i, :], x_res[:, i, :])
                    link(last)
                    for i in range(4):
                        last = V.bn_aggr(mv[:, i, :], stat[:, i, :])
                    link(last)
                    newton()
                    for i in range(4):
                        t = 4 * qh + i
                        if i >= 2:
                            dve.wait_ge(yT_ps, b * QT + t - 1)
                        V.tensor_scalar(vals[:, t % 2, :], x_res[:, i, :], mv[:, i, 0:1], nw[:, 1, i:i + 1],
                                        ALU.subtract, ALU.mult).then_inc(yn_ready, 1)
                    for i in range(4):
                        t = 4 * qh + i
                        dve.wait_ge(yT_h, b * QT + t + 1)
                        sl = (slice(None), slice(None), slice(i * P, (i + 1) * P))
                        V.tensor_tensor(yT_lo[sl], ps[:, 2 + i % 2, :].rearrange("p (a c) -> p a c", c=P), yT_hi[sl].bitcast(F32),
                                        ALU.subtract).then_inc(yT_l, 1)
                    for i in range(4):
                        t = 4 * qh + i
                        dve.wait_ge(f_ps, b * QT + t + 1)
                        if t >= 2:
                            dve.wait_ge(y_stored[t % 2], (b * 4 + t // 2) * 16)
                        else:
                            dve.wait_ge(y_stored[t % 2], b * 64)
                        V.tensor_tensor(y_out[:, t % 2, :], ps[:, 4 + i % 2, :], fb_b[:, :], ALU.add).then_inc(f_b, 1)
                    cut()


_INS = ['x', 'ctx_1024', 'mask_Bx1x1xS2_ik0', 'L0_xattn_W_q', 'L0_xattn_b_q', 'L0_xattn_W_k', 'L0_xattn_b_k',
        'L0_xattn_W_v', 'L0_xattn_b_v', 'L0_xattn_W_o', 'L0_xattn_b_o', 'L0_ffn_weight', 'L0_ffn_aux_weight1',
        'L0_ffn_aux_weight2', 'L0_ffn_bias']


def kernel(**inputs):
    import numpy as _np
    import concourse.bacc as _bacc
    from concourse import mybir as _mybir
    from concourse.bass_utils import run_bass_kernel_spmd as _run

    nc = _bacc.Bacc("TRN2", target_bir_lowering=False, num_devices=1)
    arrays, args = {}, []
    given = [(n, _np.ascontiguousarray(inputs[n])) for n in _INS]
    given += [("identity", _np.eye(P, dtype=_np.float32)), ("control_rows", control_constants())]
    for name, a in given:
        arrays[f"in_{name}"] = a
        args.append(nc.dram_tensor(f"in_{name}", a.shape, _mybir.dt.from_np(a.dtype), kind="ExternalInput").ap())
    out = nc.dram_tensor("out_0", (B, T, D), _mybir.dt.float32, kind="ExternalOutput").ap()
    build(nc, *args, out)
    r = _run(nc, [arrays], core_ids=[0])
    return r.results[0]["out_0"]
```

```python
import numpy as np
import concourse.bass as bass
from concourse import mybir
from contextlib import ExitStack

B, T, S, D, H = 4, 1024, 2048, 512, 16
DK = D // H
P = 128
KC = D // P
HG = H // 4
NT = S // P
GT = 2
GK = GT * P
QH, QW = 2, 512
QT = T // P
EPS = 1e-5
SCALE = float(1.0 / np.sqrt(np.float32(DK)))
MASKED = -1.0e30
LOWEST = -3.0e38
NROW = 192
KB = 1024

DS = bass.ds


def control_constants():
    t = np.tile(np.arange(NT), B)
    b16 = np.repeat(np.arange(B) * NT, NT)
    ev = GT * np.arange(NT // GT)
    low = np.array([[1.0 if b < j else 0.0 for b in range(B)] for j in range(B + 1)]).ravel()
    row = np.zeros((1, NROW), np.float32)
    row[0, 156:160], row[0, 160:192] = np.arange(B), np.maximum(np.arange(32) - 1, 0)
    row[0, :64], row[0, 64:128], row[0, 128:136], row[0, 136:156] = t, b16, ev, low
    return row


def build(nc, x, ctx, mask, wq, bq, wk, bk, wv, bv, wo, bo, wf, wa1, wa2, fb, ident_in, rows_in, out):
    F32, F32R, I32 = mybir.dt.float32, mybir.dt.float32r, mybir.dt.int32
    ALU, ACT, AX = mybir.AluOpType, mybir.ActivationFunctionType, mybir.AxisListType.X

    x_rows = x.rearrange("b t d -> (b t) d")
    ctx_rows = ctx.rearrange("b t d -> (b t) d")
    out_rows = out.rearrange("b t d -> (b t) d")
    mask_rows = mask.rearrange("b u v (t p) -> (b u v t) p", p=P)
    mbias_dram = nc.dram_tensor("mbias_scratch", (B * NT, P), F32, kind="Internal").ap()
    flags_dram = nc.dram_tensor("flags_scratch", (B * NT,), F32, kind="Internal").ap()
    ones_dram = nc.dram_tensor("ones_scratch", (1, H * T), F32, kind="Internal").ap()

    es = ExitStack()
    with es:
        base = (nc.sbuf_base + 31) // 32 * 32
        top = [base]

        def at(name, shape, dt, offset):
            return nc.alloc_sbuf_tensor_at(name, shape, dt, offset=offset).ap()

        def region(nbytes):
            o = top[0]
            top[0] = o + nbytes
            return o

        def own(name, shape, dt=F32):
            n = int(np.prod(shape[1:])) * 4
            return at(name, shape, dt, region((n + 31) // 32 * 32))

        wq_hi, wq_lo = own("wq_hi", [P, KC, D], F32R), own("wq_lo", [P, KC, D], F32R)
        wkT, wvT = own("wkT", [P, KC, D]), own("wvT", [P, KC, D])
        wo_hi, wo_lo = own("wo_hi", [P, KC, D], F32R), own("wo_lo", [P, KC, D], F32R)
        wf_hi, wf_lo = own("wf_hi", [P, KC, D], F32R), own("wf_lo", [P, KC, D], F32R)
        r_q, r_k = region(64 * KB), region(16 * KB)
        qs = at("qs", [P, H, T], F32R, r_q)
        raw = at("raw", [P, 7, KC, D], F32, r_q)
        a1T = at("a1T", [P, KC, D], F32, r_q + 56 * KB)
        yT_hi, yT_lo = at("yT_hi", [P, QH, KC, QW], F32R, r_q), at("yT_lo", [P, QH, KC, QW], F32R, r_q + 16 * KB)
        x_res = at("x_res", [P, QT, D], F32, r_q + 32 * KB)
        yn = at("yn", [P, 4, D], F32, r_q + 48 * KB)
        inv_x = at("inv_x", [P, 2, 4, P], F32, r_q + 56 * KB)
        ks = at("ks", [P, HG, 4, GK], F32R, r_k)
        wfT = at("wfT", [P, KC, D], F32, r_k)
        m12 = at("m12", [P, KC, D], F32, r_k + 8 * KB)
        y_out = at("y_out", [P, 4, D], F32, r_k)
        r_v = region(4 * KB)
        vals = at("vals", [P, GT, D], F32, r_v)
        r_1 = region(16 * KB)
        attn = at("attn", [P, HG, T], F32, r_1)
        xT_lo = at("xT_lo", [P, KC, T], F32R, r_1)
        r_2 = region(16 * KB)
        prob = at("prob", [P, 2, 4, QW], F32, r_2)
        xT_hi = at("xT_hi", [P, KC, T], F32R, r_2)
        r_3 = region(8 * KB)
        q_st = at("q_st", [P, 2, 2, QW], F32, r_3)
        work = at("work", [P, 4, QW], F32, r_3)
        den_sb, alpha_sb = work[:, 0, :], work[:, 1, :]
        alpha_x = work[:, 2, :].rearrange("p (c n) -> p c n", c=4)
        r_c = region(8 * KB)
        ctx_sb = at("ctx_sb", [P, GT, D], F32, r_c)
        ctxT = at("ctxT", [P, KC, GK], F32, r_c + 4 * KB)
        x_in = at("x_in", [P, 4, D], F32, r_c)
        k_st = [at("k_st0", [P, 2, 2, GK], F32, r_v), at("k_st1", [P, 2, 2, GK], F32, r_c)]
        ident = own("ident", [P, P])
        bv_b, bo_b, fb_b = own("bv_b", [P, D]), own("bo_b", [P, D]), own("fb_b", [P, D])
        m_run = own("m_run", [P, HG, 4 * QT])
        den_nat = own("den_nat", [P, HG, 4, QT])
        inv_nat = own("inv_nat", [P, HG, 4, QT])
        m_new = own("m_new", [P, 4, QT])
        m_tile = own("m_tile", [P, 4, QT])
        m_pair = own("m_pair", [P, 4, 4 * QT])
        m_dif = own("m_dif", [P, 4, QT])
        alpha_nat = own("alpha_nat", [P, 2, 4, QT])
        mT = own("mT", [2 * 4 * QT, P])
        ones32 = own("ones32", [P, 32])
        bq_c, bk_c = own("bq_c", [P, KC]), own("bk_c", [P, KC])
        stat = own("stat", [P, 4, 6])
        mv = own("mv", [P, 4, 2])
        nw = own("nw", [P, 4, 4])
        nf_all, nf_b = own("nf_all", [P, B]), own("nf_b", [P, 1])
        table = own("table", [1, 116], I32)
        assert top[0] <= 229368, top[0]
        ctl = at("ctl", [1, 2048], F32, r_3)
        mask_sb = at("mask_sb", [B * NT, P], I32, r_v)
        meq = at("meq", [B * NT, P], F32, r_v + 512)
        mbias = at("mbias", [B * NT, P], F32, r_v + 1024)
        flag = at("flag", [B * NT, 1], F32, r_v + 1536)

        ps = es.enter_context(nc.psum_tensor("ps", [P, 8, 512], F32))

        def sem(name):
            return es.enter_context(nc.semaphore(name))

        def sems(names):
            return [sem(n) for n in names.split()]

        ld_small, ld_w = sem("ld_small"), [sem(f"ld_w{n}") for n in range(7)]
        flags_set, flags_stored, flags_row, stack_rows = sems("flags_set flags_stored flags_row stack_rows")
        mask_ready, table_ready, nf_row, nf_ps = sems("mask_ready table_ready nf_row nf_ps")
        wt_ps, wt_hi, wt_done, m12_ps, m12_done, wf_ps, wf_h, wf_done = sems(
            "wt_ps wt_hi wt_done m12_ps m12_done wf_ps wf_h wf_done")
        x_loaded = [sem(f"x_loaded{n}") for n in range(4)]
        xn_ready, xT_ps, xT_h, xT_l, q_ps, q_h, q_l = sems("xn_ready xT_ps xT_h xT_l q_ps q_h q_l")
        q_stacked, ones_row = [sem(f"q_stacked{n}") for n in range(QH)], sem("ones_row")
        ctx_loaded = [sem(f"ctx_loaded{n}") for n in range(GT)]
        ctxT_ps, ctxT_a, ctxT_d, k_ps, k_h, k_l, v_ps, v_done = sems("ctxT_ps ctxT_a ctxT_d k_ps k_h k_l v_ps v_done")
        k_stacked, mask_in = [sem(f"k_stacked{n}") for n in range(2)], sem("mask_in")
        nat_ps, nat_done, m_ready, m_rows = sems("nat_ps nat_done m_ready m_rows")
        s_ps, exp_done, pv_done, den_ps, o_done, den_done = sems("s_ps exp_done pv_done den_ps o_done den_done")
        dif_ready, alpha_exp, alpha_ps, alpha_done = sems("dif_ready alpha_exp alpha_ps alpha_done")
        inv_ready, invx_done, inv_ps, scaled, a_h, a_l, oj_ps, x1_done = sems(
            "inv_ready invx_done inv_ps scaled a_h a_l oj_ps x1_done")
        xr_loaded = [sem(f"xr_loaded{n}") for n in range(QT)]
        xb_done, yn_ready, yT_ps, yT_h, yT_l, f_ps, f_b, f_tanh, y_done = sems(
            "xb_done yn_ready yT_ps yT_h yT_l f_ps f_b f_tanh y_done")
        y_stored = [sem(f"y_stored{n}") for n in range(4)]
        chain = sem("chain")
        past = {}

        def hold(eng, semaphore, value):
            eng.wait_ge(semaphore, value)
            eng.sem_inc(past[eng], 1)

        PIECES = 2 * QT
        UNITS = QH * GT

        def order():
            todo = [("nat", 0, p) for p in range(PIECES)] + [("maxT", 0, 0)]
            for hg in range(HG):
                for u in range(UNITS):
                    now = 4 * hg + u
                    heads = [("scores", now, 0), ("scores", now, 1)]
                    sums = [("weigh", now - 1, 0), ("sum", now - 1, 0)] if now else []
                    items = sums + heads if u == 0 else heads + sums
                    n, start = ((5, 0), (5, 5), (6, 10), (0, 16))[u]
                    for c, item in enumerate(items):
                        todo.append(item)
                        if hg + 1 < HG:
                            todo += [("nat", hg + 1, start + q) for q in range(n * c // len(items), n * (c + 1) // len(items))]
                        if u == 3 and item == heads[1] and hg + 1 < HG:
                            todo.append(("maxT", hg + 1, 0))
                        if u % 2 and item == heads[1] and now > 1:
                            todo.append(("denT", (now - 2) // 2, 0))
            todo += [("weigh", 15, 0), ("sum", 15, 0), ("denT", 7, 0)]
            return todo

        ORDER = order()
        TURNS = [item for item in ORDER if item[0] in ("nat", "maxT", "denT")]
        TURN = {item: n for n, item in enumerate(TURNS)}
        NTURN = len(TURNS)
        OUTS = HG * QH
        assert [x for x in ORDER if x[0] == "denT"] == [("denT", w, 0) for w in range(OUTS)]

        def groups(eng, b):
            first = eng.value_load(table[0:1, DS(b, 1)], min_val=0, max_val=B * NT // GT)
            count = eng.value_load(table[0:1, DS(b + 8, 1)], min_val=1, max_val=NT // GT)
            return first, count

        def later(eng, b, i):
            before = eng.value_load(table[0:1, DS(b + 12, 1)], min_val=0, max_val=24)
            return eng.value_load(table[0:1, DS(before + i + 80, 1)], min_val=0, max_val=31)

        def end_group(eng, b):
            return eng.value_load(table[0:1, DS(b + 1, 1)], min_val=1, max_val=B * NT // GT)

        block = es.enter_context(nc.Block())

        @block.sync
        def _(sp):
            past[sp] = sem("sp_past")

            def load_x(nb, t):
                sp.dma_start(x_in[:, t % 4, :], x_rows[DS(nb * T + t * P, P), :]).then_inc(x_loaded[t % 4], 16)

            def load_ctx(tiles):
                for j in range(GT):
                    sp.dma_start(ctx_sb[:, j, :], ctx_rows[DS(tiles[j] * P, P), :]).then_inc(ctx_loaded[j], 16)

            def stack_queries(b, m):
                for qh in range(QH):
                    hold(sp, q_l, b * 8 + 2 * m + qh + 1)
                    for g in range(4):
                        for r0, part in ((0, 0), (32, 1), (64, 0)):
                            sp.dma_start(qs[r0:r0 + 32, 4 * m + g, qh * QW:(qh + 1) * QW].bitcast(F32),
                                         q_st[32 * g:32 * g + 32, qh, part, :]).then_inc(q_stacked[qh], 16)

            def stack_keys(k, tiles):
                for half in range(2):
                    hold(sp, k_l, 2 * k + half + 1)
                    if half == 0:
                        for j in range(GT):
                            sp.dma_start(ks[96:97, :, :, j * P:(j + 1) * P].bitcast(F32).rearrange("p a b k -> p (a b) k"),
                                         mbias_dram[DS(tiles[j], 1), :].unsqueeze(1).to_broadcast([1, H, P])
                                         ).then_inc(mask_in, 16)
                    for g in range(4):
                        for r0, part in ((0, 0), (32, 0), (64, 1)):
                            sp.dma_start(ks[r0:r0 + 32, 2 * half:2 * half + 2, g, :].bitcast(F32),
                                         k_st[half][32 * g:32 * g + 32, part, :, :]).then_inc(k_stacked[half], 16)

            def tiles_of(b, i):
                return [sp.value_load(table[0:1, DS(16 + b * NT + i * GT + j, 1)], min_val=0, max_val=B * NT - 1)
                        for j in range(GT)]

            sp.dma_start(mask_sb[:, :], mask_rows).then_inc(mask_ready, 16)
            sp.dma_start(ident[:, :], ident_in).then_inc(ld_small, 16)
            sp.dma_start(ctl[0:1, 0:NROW], rows_in).then_inc(ld_small, 16)
            for n, w in enumerate((wq, wk, wv, wa1, wa2, wf, wo)):
                sp.dma_start(raw[:, n, :, :], w.rearrange("(r p) c -> p r c", p=P)).then_inc(ld_w[n], 16)
                if n == 0:
                    with nc.allow_non_contiguous_dma(reason="512 words each, once"):
                        sp.dma_start(bq_c[:, :], bq.rearrange("(m p) -> p m", p=P)).then_inc(ld_small, 16)
                        sp.dma_start(bk_c[:, :], bk.rearrange("(m p) -> p m", p=P)).then_inc(ld_small, 16)
                    for dst, src in ((bv_b, bv), (bo_b, bo), (fb_b, fb)):
                        sp.dma_start(dst[:, :], src.partition_broadcast(P)).then_inc(ld_small, 16)
                if n == 2:
                    sp.wait_ge(flags_set, 1)
                    sp.dma_start(mbias_dram, mbias[:, :]).then_inc(flags_stored, 16)
                    sp.dma_start(flags_dram.rearrange("(p a) -> p a", a=1), flag[:, :]).then_inc(flags_stored, 16)
                    sp.wait_ge(flags_stored, 32)
                    sp.dma_start(ctl[0:1, 192:256], flags_dram.rearrange("(a p) -> a p", a=1)).then_inc(flags_row, 16)
                    for t in range(4):
                        load_x(0, t)
            for t in range(4, QT):
                sp.wait_ge(xT_ps, t - 3)
                load_x(0, t)
            sp.wait_ge(table_ready, 1)
            sp.wait_ge(stack_rows, 2)
            sp.dma_start(ones_dram, qs[96:97, :, :].bitcast(F32).rearrange("p h t -> p (h t)")).then_inc(ones_row, 16)
            sp.wait_ge(ones_row, 16)
            with sp.Fori(0, B) as b:
                hold(sp, xT_ps, b * QT + QT)
                load_ctx(tiles_of(b, 0))
                first, count = groups(sp, b)
                sp.wait_ge(y_done, b * QT)
                sp.dma_start(qs[96:97, :, :].bitcast(F32).rearrange("p h t -> p (h t)"), ones_dram).then_inc(ones_row, 16)
                stack_queries(b, 0)
                tiles = tiles_of(b, 0)
                hold(sp, stack_rows, b + 3)
                stack_keys(first, tiles)
                for m in range(1, HG):
                    stack_queries(b, m)
                with sp.Fori(0, count) as i:
                    k = first + i
                    with sp.If(i > 0):
                        stack_keys(k, tiles_of(b, i))
                    for hg in range(HG):
                        sp.wait_ge(nat_done, k * NTURN + TURN["maxT", hg, 0] + 1)
                        for part in range(2):
                            sp.dma_start(qs[97 + part:98 + part, 4 * hg:4 * hg + 4, :].bitcast(F32).rearrange("p a (b c) -> p (a b) c", c=P),
                                         mT[32 * part:32 * part + 32, :]).then_inc(m_rows, 16)
                        if hg == 0:
                            with sp.If(i + 1 < count):
                                hold(sp, k_stacked[1], (k + 1) * 192)
                                load_ctx(tiles_of(b, i + 1))
                last = end_group(sp, b)
                hold(sp, o_done, last * OUTS)
                for t in range(4):
                    sp.dma_start(x_res[:, t, :], x_rows[DS(b * T + t * P, P), :]).then_inc(xr_loaded[t], 16)
                following = sp.value_load(table[0:1, DS(b + 112, 1)], min_val=0, max_val=B - 1)
                with sp.If(b < B - 1):
                    for t in range(4):
                        load_x(following, t)
                for t in range(4, QT):
                    sp.dma_start(x_res[:, t, :], x_rows[DS(b * T + t * P, P), :]).then_inc(xr_loaded[t], 16)
                with sp.If(b < B - 1):
                    for t in range(4, QT):
                        hold(sp, xT_ps, b * QT + QT + t - 3)
                        load_x(following, t)
                for t in range(QT):
                    hold(sp, y_done, b * QT + t + 1)
                    sp.dma_start(out_rows[DS(b * T + t * P, P), :], y_out[:, t % 4, :]).then_inc(y_stored[t % 4], 16)
            for n in range(4):
                sp.wait_ge(y_stored[n], B * 32)

        @block.tensor
        def _(pe):
            past[pe] = sem("pe_past")

            def transposes(out_bank, tile):
                for c in range(KC):
                    last = nc.tensor.transpose(ps[:, out_bank, c * P:(c + 1) * P], tile(c), ident[:, :])
                return last

            def product(out, pairs):
                for kc in range(KC):
                    for n, (left, right) in enumerate(pairs(kc)):
                        last = nc.tensor.matmul(out, left, right, start=kc == 0 and n == 0, stop=kc == KC - 1 and n == 2)
                return last

            def transpose_x(nb, t, free, value):
                pe.wait_ge(xn_ready, nb * QT + t + 1)
                pe.wait_ge(free, value) if t < 2 else pe.wait_ge(xT_l, nb * QT + t - 1)
                transposes(6 + t % 2, lambda c: x_in[:, t % 4, c * P:(c + 1) * P]).then_inc(xT_ps, 1)

            def queries(b, m):
                cols = slice(m * P, (m + 1) * P)
                for qh in range(QH):
                    n = 2 * m + qh
                    a = slice(qh * QW, (qh + 1) * QW)
                    pe.wait_ge(f_b, b * QT) if n < 2 else pe.wait_ge(q_l, b * 8 + n - 1)
                    product(ps[:, 4 + n % 2, :], lambda kc: ((wq_hi[:, kc, cols], xT_hi[:, kc, a]),
                                                             (wq_hi[:, kc, cols], xT_lo[:, kc, a]),
                                                             (wq_lo[:, kc, cols], xT_hi[:, kc, a]))).then_inc(q_ps, 1)

            def keys(k):
                for j in range(GT):
                    pe.wait_ge(ctx_loaded[j], k * 16 + 16)
                    last = transposes(j, lambda c: ctx_sb[:, j, c * P:(c + 1) * P])
                last.then_inc(ctxT_ps, 1)
                pe.wait_ge(ctxT_a, k + 1)
                pe.wait_ge(ctxT_d, k + 1)
                for m in range(HG):
                    for kc in range(KC):
                        last = nc.tensor.matmul(ps[:, 2 + m // 2, (m % 2) * GK:(m % 2 + 1) * GK],
                                                wkT[:, kc, m * P:(m + 1) * P], ctxT[:, kc, :],
                                                start=kc == 0, stop=kc == KC - 1)
                    if m % 2:
                        last.then_inc(k_ps, 1)

            pe.wait_ge(ld_small, 16 * 7)
            bank = 0
            for n in (0, 1, 2, 3, 5, 6):
                pe.wait_ge(ld_w[n], 16)
                for kc in range(KC):
                    if bank >= 4:
                        pe.wait_ge(wt_done, bank - 3)
                    transposes(bank % 4, lambda r: raw[:, n, r, kc * P:(kc + 1) * P]).then_inc(wt_ps, 1)
                    bank += 1
                if n == 2:
                    for t in range(4):
                        transpose_x(0, t, ld_small, 16 * 7)
                if n == 5:
                    for t in range(4, QT):
                        transpose_x(0, t, ld_small, 16 * 7)
            pe.wait_ge(wt_done, bank)
            pe.wait_ge(xT_l, QT)
            pe.wait_ge(ld_w[4], 16)
            for m in range(KC):
                for kc in range(KC):
                    last = nc.tensor.matmul(ps[:, 4 + m, :], a1T[:, kc, m * P:(m + 1) * P], raw[:, 4, kc, :],
                                            start=kc == 0, stop=kc == KC - 1)
                last.then_inc(m12_ps, 1)
            pe.wait_ge(m12_done, KC)
            for m in range(KC):
                for kc in range(KC):
                    last = nc.tensor.matmul(ps[:, 4 + m, :], wfT[:, kc, m * P:(m + 1) * P], m12[:, kc, :],
                                            start=kc == 0, stop=kc == KC - 1)
                last.then_inc(wf_ps, 1)
            pe.wait_ge(nf_row, 1)
            nc.tensor.matmul(ps[:, 0, 0:B], ctl[0:1, 1600:1728], ctl[0:1, 1728:1728 + B], start=True, stop=True).then_inc(nf_ps, 1)
            pe.wait_ge(table_ready, 1)
            pe.wait_ge(stack_rows, 2)

            with pe.Fori(0, B) as b:
                pe.wait_ge(xT_l, b * QT + QT)
                queries(b, 0)
                first, count = groups(pe, b)
                keys(first)
                for m in range(1, HG):
                    queries(b, m)
                hold(pe, q_l, b * 8 + 8)
                with pe.Fori(0, count) as i:
                    k = first + i
                    with pe.If(i > 0):
                        keys(k)
                    for what, n, p in ORDER:
                        if what in ("nat", "maxT", "denT"):
                            turn = TURN[what, n, p]
                            bank = 4 + turn % 2
                            pe.wait_ge(nat_done, k * NTURN + max(turn - 1, 0))
                        if what == "nat":
                            hg = n
                            if p == 0:
                                for qh in range(QH):
                                    pe.wait_ge(q_stacked[qh], (b * HG + hg + 1) * 192)
                                if hg % 2 == 0:
                                    pe.wait_ge(k_stacked[hg // 2], (k + 1) * 192)
                                if hg == 0:
                                    pe.wait_ge(mask_in, (k + 1) * 32)
                                    pe.wait_ge(ones_row, b * 16 + 32)
                                    pe.wait_ge(o_done, k * OUTS)
                                    pe.wait_ge(den_done, k * OUTS)
                            qt, pair = divmod(p, 2)
                            for s in range(2):
                                g = 2 * pair + s
                                last = nc.tensor.matmul(ps[:, bank, s * GK:(s + 1) * GK],
                                                        qs[0:97, 4 * hg + g, qt * P:(qt + 1) * P],
                                                        ks[0:97, hg, g, :], start=True, stop=True)
                            last.then_inc(nat_ps, 1)
                            if hg == 0 and p % 2:
                                j, kc = divmod(p // 2, KC)
                                last = nc.tensor.matmul(ps[:, 6 + j, :], ctxT[:, kc, j * P:(j + 1) * P], wvT[:, kc, :],
                                                        start=kc == 0, stop=kc == KC - 1)
                                if kc == KC - 1:
                                    last.then_inc(v_ps, 1)
                        elif what == "maxT":
                            pe.wait_ge(m_ready, k * HG + n + 1)
                            nc.tensor.transpose(ps[:, bank, 0:P], m_pair[:, :, :].rearrange("p a b -> p (a b)"),
                                                ident[:, :]).then_inc(nat_ps, 1)
                        elif what == "denT":
                            pe.wait_ge(den_done, k * OUTS + n + 1)
                            transposes(bank, lambda c: den_sb[:, c * P:(c + 1) * P]).then_inc(nat_ps, 1)
                        elif what == "scores":
                            hg, qh, j = n // 4, n % 4 // GT, n % GT
                            if n % 4 == 0 and p == 0:
                                pe.wait_ge(m_rows, (k * HG + hg + 1) * 32)
                            pe.wait_ge(exp_done, k * 32 + max(2 * n + p - 1, 0))
                            for s in range(2):
                                g = 2 * p + s
                                last = nc.tensor.matmul(ps[:, 2 * p + s, :], ks[0:99, hg, g, j * P:(j + 1) * P],
                                                        qs[0:99, 4 * hg + g, qh * QW:(qh + 1) * QW],
                                                        start=True, stop=True)
                            last.then_inc(s_ps, 1)
                        elif what == "weigh":
                            j, w = n % GT, n // GT
                            if n == 0:
                                pe.wait_ge(v_done, k * GT + GT)
                            if j == 0:
                                hold(pe, o_done, k * OUTS + w)
                                with pe.If(i > 0):
                                    late = later(pe, b, i)
                                    pe.wait_ge(alpha_exp, late * OUTS + w + 1)
                                    transposes(6, lambda c: alpha_x[:, c, :]).then_inc(alpha_ps, 1)
                                    hold(pe, alpha_done, late * OUTS + w + 1)
                            pe.wait_ge(exp_done, k * 32 + 2 * n + 2)
                            for g in range(4):
                                h = 4 * (n // 4) + g
                                last = nc.tensor.matmul(ps[32 * g:32 * g + 32, 6, :], vals[:, j, h * DK:(h + 1) * DK],
                                                        prob[:, n % 2, g, :], start=j == 0, stop=j == GT - 1)
                            last.then_inc(pv_done, 1)
                        elif what == "sum":
                            j, w = n % GT, n // GT
                            if j == 0:
                                pe.wait_ge(den_done, k * OUTS + w)
                            for g in range(4):
                                last = nc.tensor.matmul(ps[32 * g:32 * g + 32, 7, :], ones32[:, :],
                                                        prob[:, n % 2, g, :], start=j == 0, stop=j == GT - 1)
                            last.then_inc(den_ps, 1)

                def inverse(n):
                    pe.wait_ge(invx_done, b * OUTS + n + 1)
                    if n >= 2:
                        pe.wait_ge(scaled, b * OUTS + n - 1)
                    transposes(6 + n % 2, lambda c: inv_x[:, n % 2, c, :]).then_inc(inv_ps, 1)

                def left(t):
                    qh, i = divmod(t, 4)
                    return qh, slice(i * P, (i + 1) * P)

                def out_proj(t):
                    qh, rows = left(t)
                    if t % 4 == 0:
                        pe.wait_ge(a_l, b * OUTS + 4 * qh + 4)
                    if t >= 2:
                        pe.wait_ge(x1_done, b * QT + t - 1)
                    product(ps[:, t % 2, :], lambda kc: ((yT_hi[:, qh, kc, rows], wo_hi[:, kc, :]),
                                                         (yT_hi[:, qh, kc, rows], wo_lo[:, kc, :]),
                                                         (yT_lo[:, qh, kc, rows], wo_hi[:, kc, :]))).then_inc(oj_ps, 1)

                def transpose_y(t):
                    pe.wait_ge(yn_ready, b * QT + t + 1)
                    if t >= 2:
                        pe.wait_ge(yT_l, b * QT + t - 1)
                    transposes(2 + t % 2, lambda c: yn[:, t % 4, c * P:(c + 1) * P]).then_inc(yT_ps, 1)

                def ffn(t):
                    qh, rows = left(t)
                    pe.wait_ge(yT_l, b * QT + t + 1)
                    if t >= 2:
                        pe.wait_ge(f_b, b * QT + t - 1)
                    product(ps[:, 4 + t % 2, :], lambda kc: ((yT_hi[:, qh, kc, rows], wf_hi[:, kc, :]),
                                                             (yT_hi[:, qh, kc, rows], wf_lo[:, kc, :]),
                                                             (yT_lo[:, qh, kc, rows], wf_hi[:, kc, :]))).then_inc(f_ps, 1)

                def next_x(half):
                    with pe.If(b < B - 1):
                        for t in range(4 * half, 4 * half + 4):
                            transpose_x(b + 1, t, scaled, b * OUTS + OUTS)

                for n in range(4):
                    inverse(n)
                for t in range(4):
                    out_proj(t)
                    inverse(4 + t)
                for t in range(4, QT):
                    out_proj(t)
                for t in range(4):
                    transpose_y(t)
                next_x(0)
                ffn(0)
                ffn(1)
                for t in range(4, QT):
                    transpose_y(t)
                ffn(2)
                ffn(3)
                next_x(1)
                for t in range(4, QT):
                    ffn(t)

        @block.scalar
        def _(act):
            def high_x(nb, t):
                act.wait_ge(xT_ps, nb * QT + t + 1)
                nc.scalar.activation(xT_hi[:, :, t * P:(t + 1) * P], ps[:, 6 + t % 2, :].rearrange("p (a c) -> p a c", c=P),
                                     ACT.Copy).then_inc(xT_h, 1)

            def high_q(b, m):
                for qh in range(QH):
                    n = 2 * m + qh
                    act.wait_ge(q_ps, b * 8 + n + 1)
                    act.wait_ge(q_stacked[qh], (b * HG + m) * 192)
                    nc.scalar.activation(q_st[:, qh, 0, :].bitcast(F32R), ps[:, 4 + n % 2, :], ACT.Identity,
                                         bias=bq_c[:, m:m + 1]).then_inc(q_h, 1)

            def high_k(k):
                act.wait_ge(ctxT_ps, k + 1)
                nc.scalar.activation(ctxT[:, :, 0:P], ps[:, 0, :].rearrange("p (a c) -> p a c", c=P), ACT.Copy).then_inc(ctxT_a, 1)
                for m in range(HG):
                    if m % 2 == 0:
                        act.wait_ge(k_ps, k * 2 + m // 2 + 1)
                    nc.scalar.activation(k_st[m // 2][:, 0, m % 2, :].bitcast(F32R), ps[:, 2 + m // 2, (m % 2) * GK:(m % 2 + 1) * GK],
                                         ACT.Identity, bias=bk_c[:, m:m + 1]).then_inc(k_h, 1)

            bank = 0
            for n in (0, 1, 2, 3, 5, 6):
                for kc in range(KC):
                    if n in (0, 6):
                        act.wait_ge(wt_ps, bank + 1)
                        nc.scalar.activation((wq_hi if n == 0 else wo_hi)[:, kc, :], ps[:, bank % 4, :], ACT.Copy).then_inc(wt_hi, 1)
                    bank += 1
                if n in (2, 5):
                    for t in range(4 * (n == 5), 4 * (n == 5) + 4):
                        high_x(0, t)
            for m in range(KC):
                act.wait_ge(m12_ps, m + 1)
                nc.scalar.activation(m12[:, m, :], ps[:, 4 + m, :], ACT.Copy).then_inc(m12_done, 1)
            for m in range(KC):
                act.wait_ge(wf_ps, m + 1)
                nc.scalar.activation(wf_hi[:, m, :], ps[:, 4 + m, :], ACT.Copy).then_inc(wf_h, 1)
            act.wait_ge(table_ready, 1)
            act.wait_ge(ld_small, 16 * 7)

            with act.Fori(0, B) as b:
                high_q(b, 0)
                first, count = groups(act, b)
                high_k(first)
                for m in range(1, HG):
                    high_q(b, m)
                with act.Fori(0, count) as i:
                    k = first + i
                    with act.If(i > 0):
                        high_k(k)
                    for what, n, p in ORDER:
                        if what == "scores":
                            hg, w = n // 4, n // GT
                            if n % GT == 0 and p == 0:
                                with act.If(i > 0):
                                    late = later(act, b, i)
                                    act.wait_ge(dif_ready, late * HG + hg + 1)
                                    act.wait_ge(alpha_ps, late * OUTS + w)
                                    if w % QH == 0:
                                        nc.scalar.activation(alpha_nat[:, hg % 2, :, :], m_dif[:, :, :], ACT.Exp, scale=SCALE)
                                    for c in range(4):
                                        qt = 4 * (w % QH) + c
                                        last = nc.scalar.activation(
                                            alpha_x[:, c, :].rearrange("p (g r) -> p g r", r=32),
                                            m_dif[:, :, qt:qt + 1].to_broadcast([P, 4, 32]), ACT.Exp, scale=SCALE)
                                    last.then_inc(alpha_exp, 1)
                            act.wait_ge(s_ps, k * 32 + 2 * n + p + 1)
                            act.wait_ge(den_ps, k * 16 + max(n - 1, 0))
                            nc.scalar.activation(prob[:, n % 2, 2 * p:2 * p + 2, :], ps[:, 2 * p:2 * p + 2, :],
                                                 ACT.Exp, scale=SCALE).then_inc(exp_done, 1)
                        elif what == "sum" and n % GT == GT - 1:
                            w = n // GT
                            act.wait_ge(den_ps, k * 16 + n + 1)
                            if w:
                                act.wait_ge(nat_ps, k * NTURN + TURN["denT", w - 1, 0] + 1)
                            nc.scalar.activation(den_sb, ps[:, 7, :], ACT.Copy).then_inc(den_done, 1)

                def spread(n):
                    qh, hg = divmod(n, 4)
                    if n == 0:
                        act.wait_ge(inv_ready, b + 1)
                    if n >= 2:
                        act.wait_ge(inv_ps, b * OUTS + n - 1)
                    nc.scalar.activation(inv_x[:, n % 2, :, :].rearrange("p c (g r) -> p c g r", r=32),
                                         inv_nat[:, hg, :, 4 * qh:4 * qh + 4].rearrange("p g c -> p c g").unsqueeze(3).to_broadcast([P, 4, 4, 32]),
                                         ACT.Copy).then_inc(invx_done, 1)

                def high_a(n):
                    qh, hg = divmod(n, 4)
                    act.wait_ge(scaled, b * OUTS + n + 1)
                    nc.scalar.activation(yT_hi[:, qh, hg, :], attn[:, hg, qh * QW:(qh + 1) * QW], ACT.Copy).then_inc(a_h, 1)

                def high_y(t):
                    act.wait_ge(yT_ps, b * QT + t + 1)
                    nc.scalar.activation(yT_hi[:, t // 4, :, (t % 4) * P:(t % 4 + 1) * P],
                                         ps[:, 2 + t % 2, :].rearrange("p (a c) -> p a c", c=P), ACT.Copy).then_inc(yT_h, 1)

                def tanh(t):
                    act.wait_ge(f_b, b * QT + t + 1)
                    nc.scalar.activation(y_out[:, t % 4, :], y_out[:, t % 4, :], ACT.Tanh).then_inc(f_tanh, 1)

                def next_x(half):
                    with act.If(b < B - 1):
                        for t in range(4 * half, 4 * half + 4):
                            high_x(b + 1, t)

                spread(0)
                spread(1)
                for n in range(OUTS):
                    high_a(n)
                    if n + 2 < OUTS:
                        spread(n + 2)
                for t in range(4):
                    high_y(t)
                next_x(0)
                tanh(0)
                tanh(1)
                for t in range(4, QT):
                    high_y(t)
                tanh(2)
                tanh(3)
                next_x(1)
                for t in range(4, QT):
                    tanh(t)

        @block.gpsimd
        def _(pool):
            past[pool] = sem("pool_past")
            pool.wait_ge(wf_ps, KC)
            nc.gpsimd.memset(qs[96:P, :, :].bitcast(F32), 1.0).then_inc(stack_rows, 1)
            pool.wait_ge(stack_rows, 1)
            nc.gpsimd.memset(ks[96:P, :, :, :].bitcast(F32), -1.0).then_inc(stack_rows, 1)
            pool.wait_ge(stack_rows, 2)
            with pool.Fori(0, B) as b:
                for n in range(4):
                    hold(pool, y_stored[n], b * 32)
                nc.gpsimd.memset(ks[96:P, 0:2, :, :].bitcast(F32), -1.0).then_inc(stack_rows, 1)
                for t in range(QT):
                    pool.wait_ge(xr_loaded[t], b * 16 + 16)
                    nc.gpsimd.tensor_tensor(x_res[:, t, :], x_res[:, t, :], bo_b[:, :], ALU.add).then_inc(xb_done, 1)
                for t in range(QT):
                    pool.wait_ge(f_tanh, b * QT + t + 1)
                    nc.gpsimd.tensor_tensor(y_out[:, t % 4, :], y_out[:, t % 4, :], x_res[:, t, :], ALU.add).then_inc(y_done, 1)

        @block.vector
        def _(dve):
            past[dve] = sem("dve_past")
            links = [0]

            def link(ins):
                links[0] += 1
                ins.then_inc(chain, 1)
                dve.wait_ge(chain, links[0])

            def cut():
                links[0] = 0
                dve.sem_clear(chain)

            V = nc.vector

            dve.wait_ge(mask_ready, 16)
            link(V.tensor_scalar(meq[:, :], mask_sb[:, :], 0.0, None, ALU.is_equal))
            V.tensor_scalar(mbias[:, :], meq[:, :], MASKED, None, ALU.mult)
            link(V.tensor_reduce(flag[:, :], meq[:, :], AX, ALU.min))
            V.memset(ones32[:, :], 1.0)
            V.memset(ctl[0:1, 1600:1728], 1.0).then_inc(flags_set, 1)

            bank = 0
            def weights(ns):
                nonlocal bank
                for n in ns:
                    for kc in range(KC):
                        dve.wait_ge(wt_ps, bank + 1)
                        src = ps[:, bank % 4, :]
                        if n in (0, 6):
                            hi, lo = (wq_hi, wq_lo) if n == 0 else (wo_hi, wo_lo)
                            dve.wait_ge(wt_hi, (0 if n == 0 else 4) + kc + 1)
                            V.tensor_tensor(lo[:, kc, :], src, hi[:, kc, :].bitcast(F32), ALU.subtract).then_inc(wt_done, 1)
                        else:
                            dst = {1: wkT, 2: wvT, 3: a1T, 5: wfT}[n]
                            V.tensor_copy(dst[:, kc, :], src).then_inc(wt_done, 1)
                        bank += 1

            def newton():
                a, y, t_, n_ = (nw[:, q, :] for q in range(4))
                link(V.tensor_scalar(a, mv[:, :, 1], EPS, None, ALU.add))
                link(V.tensor_scalar(n_.bitcast(I32), a.bitcast(I32), 1, None, ALU.arith_shift_right))
                link(V.tensor_scalar(y.bitcast(I32), n_.bitcast(I32), -1.0, float(0x5F3759DF), ALU.mult, ALU.add))
                for _ in range(3):
                    link(V.scalar_tensor_tensor(t_, y, -0.5, y, ALU.mult, ALU.mult))
                    link(V.tensor_tensor(t_, t_, a, ALU.mult))
                    link(V.scalar_tensor_tensor(y, t_, 1.5, y, ALU.add, ALU.mult))

            def moments(last):
                link(last)
                for i in range(4):
                    last = V.bn_aggr(mv[:, i, :], stat[:, i, :])
                link(last)
                newton()

            def norm_x(nb, half):
                for i in range(4):
                    dve.wait_ge(x_loaded[i], (nb * 2 + half + 1) * 16)
                    last = V.bn_stats(stat[:, i, :], x_in[:, i, :])
                moments(last)
                for i in range(4):
                    V.tensor_scalar(x_in[:, i, :], x_in[:, i, :], mv[:, i, 0:1], nw[:, 1, i:i + 1],
                                    ALU.subtract, ALU.mult).then_inc(xn_ready, 1)

            def low_x(nb, half):
                for t in range(4 * half, 4 * half + 4):
                    dve.wait_ge(xT_h, nb * QT + t + 1)
                    cols = slice(t * P, (t + 1) * P)
                    V.tensor_tensor(xT_lo[:, :, cols], ps[:, 6 + t % 2, :].rearrange("p (a c) -> p a c", c=P),
                                    xT_hi[:, :, cols].bitcast(F32), ALU.subtract).then_inc(xT_l, 1)

            def low_q(b, m):
                for qh in range(QH):
                    n = 2 * m + qh
                    dve.wait_ge(q_h, b * 8 + n + 1)
                    V.scalar_tensor_tensor(q_st[:, qh, 1, :].bitcast(F32R), ps[:, 4 + n % 2, :], bq_c[:, m:m + 1],
                                           q_st[:, qh, 0, :], ALU.add, ALU.subtract).then_inc(q_l, 1)

            def low_k(k):
                dve.wait_ge(ctxT_ps, k + 1)
                V.tensor_copy(ctxT[:, :, P:2 * P], ps[:, 1, :].rearrange("p (a c) -> p a c", c=P)).then_inc(ctxT_d, 1)
                for m in range(HG):
                    if m % 2 == 0:
                        dve.wait_ge(k_h, k * HG + m + 2)
                    ins = V.scalar_tensor_tensor(k_st[m // 2][:, 1, m % 2, :].bitcast(F32R),
                                                 ps[:, 2 + m // 2, (m % 2) * GK:(m % 2 + 1) * GK],
                                                 bk_c[:, m:m + 1], k_st[m // 2][:, 0, m % 2, :], ALU.add, ALU.subtract)
                    if m % 2:
                        ins.then_inc(k_l, 1)

            weights((0,))
            dve.wait_ge(flags_row, 16)
            dve.wait_ge(ld_small, 16 * 7)
            tno, b16 = ctl[0:1, 0:64], ctl[0:1, 64:128]
            ev, low = ctl[0:1, 128:136], ctl[0:1, 136:156]
            e, key, rank = ctl[0:1, 192:256], ctl[0:1, 256:320], ctl[0:1, 320:384]
            perm, n_act, grp, gt8 = ctl[0:1, 384:448], ctl[0:1, 448:452], ctl[0:1, 456:460], ctl[0:1, 464:496]
            act_t, cum5, acc, val = ctl[0:1, 1536:1600], ctl[0:1, 1760:1780], ctl[0:1, 1784:1789], ctl[0:1, 1792:1796]
            cmp4 = ctl[0:1, 512:1536].rearrange("p (b t u) -> p b t u", b=B, t=NT)
            link(V.scalar_tensor_tensor(key, e, float(NT), tno, ALU.mult, ALU.add))
            k3 = key.rearrange("p (b t) -> p b t", b=B)
            link(V.tensor_tensor(cmp4, k3.unsqueeze(2).to_broadcast([1, B, NT, NT]),
                                 k3.unsqueeze(3).to_broadcast([1, B, NT, NT]), ALU.is_lt))
            link(V.tensor_reduce(rank.rearrange("p (b t) -> p b t", b=B), cmp4, AX, ALU.add))
            r3 = rank.rearrange("p (b t) -> p b t", b=B)
            t3 = tno.rearrange("p (b t) -> p b t", b=B)
            link(V.tensor_tensor(cmp4, r3.unsqueeze(2).to_broadcast([1, B, NT, NT]),
                                 t3.unsqueeze(3).to_broadcast([1, B, NT, NT]), ALU.is_equal))
            link(V.tensor_tensor(cmp4, cmp4, t3.unsqueeze(2).to_broadcast([1, B, NT, NT]), ALU.mult))
            link(V.tensor_reduce(perm.rearrange("p (b t) -> p b t", b=B), cmp4, AX, ALU.add))
            V.tensor_tensor(table[0:1, 16:80], perm, b16, ALU.add)
            link(V.tensor_scalar(act_t, e, -1.0, 1.0, ALU.mult, ALU.add))
            link(V.tensor_reduce(n_act, act_t.rearrange("p (b t) -> p b t", b=B), AX, ALU.add))
            g3 = gt8.rearrange("p (b i) -> p b i", b=B)
            link(V.tensor_tensor(g3, n_act.unsqueeze(2).to_broadcast([1, B, 8]), ev.unsqueeze(1).to_broadcast([1, B, 8]), ALU.is_gt))
            link(V.tensor_reduce(grp, g3, AX, ALU.add))
            link(V.tensor_scalar(grp, grp, 1.0, None, ALU.max))
            V.tensor_copy(table[0:1, 8:12], grp)
            c3 = cum5.rearrange("p (j b) -> p j b", b=B)
            link(V.tensor_tensor(c3, grp.unsqueeze(1).to_broadcast([1, B + 1, B]), low.rearrange("p (j b) -> p j b", b=B), ALU.mult))
            link(V.tensor_reduce(acc, c3, AX, ALU.add))
            V.tensor_copy(table[0:1, 80:112], ctl[0:1, 160:192])
            V.tensor_scalar(table[0:1, 112:116], ctl[0:1, 156:160], 1.0, B - 1.0, ALU.add, ALU.min)
            V.tensor_tensor(table[0:1, 12:16], acc[:, 0:4], ctl[0:1, 156:160], ALU.subtract)
            link(V.tensor_copy(table[0:1, 0:5], acc))
            link(V.tensor_scalar(val, n_act, 1.0, None, ALU.min))
            link(V.reciprocal(ctl[0:1, 1740:1744], val))
            V.tensor_tensor(ctl[0:1, 1728:1732], val, ctl[0:1, 1740:1744], ALU.mult).then_inc(nf_row, 1)

            weights((1, 2))
            norm_x(0, 0)
            low_x(0, 0)
            weights((3, 5))
            norm_x(0, 1)
            low_x(0, 1)
            weights((6,))
            for m in range(KC):
                dve.wait_ge(wf_h, m + 1)
                V.tensor_tensor(wf_lo[:, m, :], ps[:, 4 + m, :], wf_hi[:, m, :].bitcast(F32), ALU.subtract).then_inc(wf_done, 1)
            dve.wait_ge(nf_ps, 1)
            link(V.tensor_copy(nf_all[:, :], ps[:, 0, 0:B]))
            cut()
            V.memset(m_pair[:, :, :], 0.0).then_inc(table_ready, 1)

            with dve.Fori(0, B) as b:
                low_q(b, 0)
                first, count = groups(dve, b)
                low_k(first)
                for m in range(1, HG):
                    low_q(b, m)
                V.memset(m_run[:, :, :], LOWEST)
                V.memset(den_nat[:, :, :, :], 0.0)
                link(V.tensor_copy(nf_b[:, :], nf_all[:, DS(b, 1)]))
                cut()
                with dve.Fori(0, count) as i:
                    k = first + i

                    def maxima(hg):
                        dve.wait_ge(nat_done, k * NTURN + TURN["nat", hg, PIECES - 1] + 1)
                        run = m_run[:, hg, :].rearrange("p (a b) -> p a b", b=QT)
                        link(V.tensor_tensor(m_new[:, :, :], m_tile[:, :, :], run, ALU.max))
                        with dve.If(i > 0):
                            late = later(dve, b, i)
                            dve.wait_ge(alpha_exp, late * OUTS + hg * QH)
                            V.tensor_tensor(m_dif[:, :, :], run, m_new[:, :, :], ALU.subtract).then_inc(dif_ready, 1)
                            hold(dve, dif_ready, late * HG + hg + 1)
                        V.tensor_copy(run, m_new[:, :, :])
                        hi, lo = m_pair[:, 0, :], m_pair[:, 1, :]
                        new = m_new[:, :, :].rearrange("p a b -> p (a b)")
                        link(V.tensor_copy(hi.bitcast(F32R), new))
                        V.tensor_tensor(lo, new, hi, ALU.subtract).then_inc(m_ready, 1)
                        cut()

                    with dve.If(i > 0):
                        low_k(k)
                    for what, n, p in ORDER:
                        if what in ("nat", "maxT", "denT"):
                            turn = TURN[what, n, p]
                            src = ps[:, 4 + turn % 2, :]
                        if what in ("nat", "maxT"):
                            dve.wait_ge(nat_ps, k * NTURN + turn + 1)
                        if what == "nat":
                            qt, pair = divmod(p, 2)
                            V.tensor_reduce(m_tile[:, 2 * pair:2 * pair + 2, qt:qt + 1].rearrange("p a b -> p (a b)"),
                                            src.rearrange("p (a c) -> p a c", c=GK), AX, ALU.max).then_inc(nat_done, 1)
                            if n == 0 and p in (9, 15):
                                j = 0 if p == 9 else 1
                                dve.wait_ge(v_ps, k * GT + j + 1)
                                V.tensor_tensor(vals[:, j, :], ps[:, 6 + j, :], bv_b[:, :], ALU.add).then_inc(v_done, 1)
                            if p == PIECES - 1:
                                maxima(n)
                        elif what == "maxT":
                            if n:
                                dve.wait_ge(m_rows, (k * HG + n) * 32)
                            V.tensor_copy(mT[:, :], src[0:64, 0:P]).then_inc(nat_done, 1)
                        elif what == "denT":
                            hg, qh = divmod(n, QH)
                            den = den_nat[:, hg, :, 4 * qh:4 * qh + 4]
                            hold(dve, nat_ps, k * NTURN + turn + 1)
                            with dve.If(i > 0):
                                V.tensor_tensor(den, den, alpha_nat[:, hg % 2, :, 4 * qh:4 * qh + 4], ALU.mult).then_inc(chain, 1)
                                dve.wait_ge(chain, 1)
                                dve.sem_clear(chain)
                            V.tensor_tensor(den, src.rearrange("p (c g r) -> p g c r", c=4, r=32)[:, :, :, 0], den,
                                            ALU.add).then_inc(nat_done, 1)
                        elif what == "weigh" and n % GT == 0:
                            with dve.If(i > 0):
                                late = later(dve, b, i)
                                dve.wait_ge(alpha_ps, late * OUTS + n // GT + 1)
                                V.tensor_copy(alpha_sb, ps[:, 6, :]).then_inc(alpha_done, 1)
                        elif what == "weigh":
                            w = n // GT
                            hg, qh = divmod(w, QH)
                            dst = attn[:, hg, qh * QW:(qh + 1) * QW]
                            hold(dve, pv_done, k * 16 + n + 1)
                            with dve.If(i > 0):
                                V.tensor_tensor(dst, dst, alpha_sb, ALU.mult).then_inc(chain, 1)
                                dve.wait_ge(chain, 1)
                                dve.sem_clear(chain)
                                V.tensor_tensor(dst, ps[:, 6, :], dst, ALU.add).then_inc(o_done, 1)
                            with dve.If(i < 1):
                                V.tensor_copy(dst, ps[:, 6, :]).then_inc(o_done, 1)

                def scale_a(n):
                    qh, hg = divmod(n, 4)
                    dst = attn[:, hg, qh * QW:(qh + 1) * QW]
                    dve.wait_ge(inv_ps, b * OUTS + n + 1)
                    V.tensor_tensor(dst, ps[:, 6 + n % 2, :], dst, ALU.mult).then_inc(scaled, 1)

                def low_a(n):
                    qh, hg = divmod(n, 4)
                    dve.wait_ge(a_h, b * OUTS + n + 1)
                    V.tensor_tensor(yT_lo[:, qh, hg, :], attn[:, hg, qh * QW:(qh + 1) * QW], yT_hi[:, qh, hg, :].bitcast(F32),
                                    ALU.subtract).then_inc(a_l, 1)

                def residual(t):
                    dve.wait_ge(oj_ps, b * QT + t + 1)
                    dve.wait_ge(xb_done, b * QT + t + 1)
                    V.tensor_tensor(x_res[:, t, :], ps[:, t % 2, :], x_res[:, t, :], ALU.add).then_inc(x1_done, 1)
                    dve.wait_ge(x1_done, b * QT + t + 1)
                    return V.bn_stats(stat[:, t % 4, :], x_res[:, t, :])

                def norm_y(half, last):
                    moments(last)
                    for t in range(4 * half, 4 * half + 4):
                        if half:
                            dve.wait_ge(yT_ps, b * QT + t - 3)
                        V.tensor_scalar(yn[:, t % 4, :], x_res[:, t, :], mv[:, t % 4, 0:1], nw[:, 1, t % 4:t % 4 + 1],
                                        ALU.subtract, ALU.mult).then_inc(yn_ready, 1)

                def low_y(t):
                    dve.wait_ge(yT_h, b * QT + t + 1)
                    cols = slice((t % 4) * P, (t % 4 + 1) * P)
                    V.tensor_tensor(yT_lo[:, t // 4, :, cols], ps[:, 2 + t % 2, :].rearrange("p (a c) -> p a c", c=P),
                                    yT_hi[:, t // 4, :, cols].bitcast(F32), ALU.subtract).then_inc(yT_l, 1)

                def ffn_bias(t):
                    dve.wait_ge(f_ps, b * QT + t + 1)
                    dve.wait_ge(y_stored[t % 4], (2 * b + t // 4) * 16)
                    V.tensor_tensor(y_out[:, t % 4, :], ps[:, 4 + t % 2, :], fb_b[:, :], ALU.add).then_inc(f_b, 1)

                def next_x(norm, low):
                    with dve.If(b < B - 1):
                        if norm is not None:
                            norm_x(b + 1, norm)
                            cut()
                        if low is not None:
                            low_x(b + 1, low)

                hold(dve, nat_done, end_group(dve, b) * NTURN)
                link(V.reciprocal(inv_nat[:, :, :, :], den_nat[:, :, :, :]))
                V.tensor_scalar(inv_nat[:, :, :, :], inv_nat[:, :, :, :], nf_b[:, 0:1], None, ALU.mult).then_inc(inv_ready, 1)
                for n in range(4):
                    scale_a(n)
                    if n:
                        low_a(n - 1)
                low_a(3)
                for t in range(4):
                    last = residual(t)
                    scale_a(4 + t)
                    low_a(4 + t)
                norm_y(0, last)
                cut()
                next_x(0, None)
                for t in range(4, QT):
                    last = residual(t)
                for t in range(4):
                    low_y(t)
                norm_y(1, last)
                cut()
                next_x(None, 0)
                ffn_bias(0)
                ffn_bias(1)
                next_x(1, None)
                for t in range(4, QT):
                    low_y(t)
                ffn_bias(2)
                ffn_bias(3)
                next_x(None, 1)
                for t in range(4, QT):
                    ffn_bias(t)


_INS = ['x', 'ctx_1024', 'mask_Bx1x1xS2_ik0', 'L0_xattn_W_q', 'L0_xattn_b_q', 'L0_xattn_W_k', 'L0_xattn_b_k',
        'L0_xattn_W_v', 'L0_xattn_b_v', 'L0_xattn_W_o', 'L0_xattn_b_o', 'L0_ffn_weight', 'L0_ffn_aux_weight1',
        'L0_ffn_aux_weight2', 'L0_ffn_bias']


def kernel(**inputs):
    import numpy as _np
    import concourse.bacc as _bacc
    from concourse import mybir as _mybir
    from concourse.bass_utils import run_bass_kernel_spmd as _run

    nc = _bacc.Bacc("TRN2", target_bir_lowering=False, num_devices=1)
    arrays, args = {}, []
    given = [(n, _np.ascontiguousarray(inputs[n])) for n in _INS]
    given += [("identity", _np.eye(P, dtype=_np.float32)), ("control_rows", control_constants())]
    for name, a in given:
        arrays[f"in_{name}"] = a
        args.append(nc.dram_tensor(f"in_{name}", a.shape, _mybir.dt.from_np(a.dtype), kind="ExternalInput").ap())
    out = nc.dram_tensor("out_0", (B, T, D), _mybir.dt.float32, kind="ExternalOutput").ap()
    build(nc, *args, out)
    r = _run(nc, [arrays], core_ids=[0])
    return r.results[0]["out_0"]
```

```python
import numpy as np
import concourse.bass as bass
from concourse import mybir
from contextlib import ExitStack

B, T, S, D, H = 4, 1024, 2048, 512, 16
DK = D // H
P = 128
KC = D // P
HG = H // 4
NT = S // P
GT = 2
GK = GT * P
QH, QW = 2, 512
QT = T // P
EPS = 1e-5
SCALE = float(1.0 / np.sqrt(np.float32(DK)))
MASKED = -1.0e30
LOWEST = -3.0e38
NROW = 192
KB = 1024

DS = bass.ds


def control_constants():
    t = np.tile(np.arange(NT), B)
    b16 = np.repeat(np.arange(B) * NT, NT)
    ev = GT * np.arange(NT // GT)
    low = np.array([[1.0 if b < j else 0.0 for b in range(B)] for j in range(B + 1)]).ravel()
    row = np.zeros((1, NROW), np.float32)
    row[0, 156:160], row[0, 160:192] = np.arange(B), np.maximum(np.arange(32) - 1, 0)
    row[0, :64], row[0, 64:128], row[0, 128:136], row[0, 136:156] = t, b16, ev, low
    return row


def selections():
    a = np.zeros((P, 4, 8, DK), np.float32)
    for g in range(4):
        for block in (0, 2, 3, 6):
            a[g * DK:(g + 1) * DK, g, block] = np.eye(DK, dtype=np.float32)
    return a.reshape(P, 4, 8 * DK)


Q_PLACES, K_PLACES = (0, 5), (2, 4)


def build(nc, x, ctx, mask, wq, bq, wk, bk, wv, bv, wo, bo, wf, wa1, wa2, fb, ident_in, select_in, ones_in, rows_in, out):
    F32, F32R, I32 = mybir.dt.float32, mybir.dt.float32r, mybir.dt.int32
    ALU, ACT, AX = mybir.AluOpType, mybir.ActivationFunctionType, mybir.AxisListType.X

    x_rows = x.rearrange("b t d -> (b t) d")
    ctx_rows = ctx.rearrange("b t d -> (b t) d")
    out_rows = out.rearrange("b t d -> (b t) d")
    mask_rows = mask.rearrange("b u v (t p) -> (b u v t) p", p=P)
    mbias_dram = nc.dram_tensor("mbias_scratch", (B * NT, P), F32, kind="Internal").ap()
    ones_dram = nc.dram_tensor("ones_scratch", (1, H * T), F32, kind="Internal").ap()
    select_dram = nc.dram_tensor("select_scratch", (P, 4, 8 * DK), F32, kind="Internal").ap()
    flags_dram = nc.dram_tensor("flags_scratch", (B * NT,), F32, kind="Internal").ap()

    es = ExitStack()
    with es:
        base = (nc.sbuf_base + 31) // 32 * 32
        top = [base]

        def at(name, shape, dt, offset):
            return nc.alloc_sbuf_tensor_at(name, shape, dt, offset=offset).ap()

        def region(nbytes):
            o = top[0]
            top[0] = o + nbytes
            return o

        def own(name, shape, dt=F32):
            n = int(np.prod(shape[1:])) * 4
            return at(name, shape, dt, region((n + 31) // 32 * 32))

        wq_hi, wq_lo = own("wq_hi", [P, KC, D], F32R), own("wq_lo", [P, KC, D], F32R)
        wkT, wvT = own("wkT", [P, KC, D]), own("wvT", [P, KC, D])
        wo_hi, wo_lo = own("wo_hi", [P, KC, D], F32R), own("wo_lo", [P, KC, D], F32R)
        wf_hi, wf_lo = own("wf_hi", [P, KC, D], F32R), own("wf_lo", [P, KC, D], F32R)
        r_q, r_k = region(64 * KB), region(16 * KB)
        qs = at("qs", [P, H, T], F32R, r_q)
        raw = at("raw", [P, 7, KC, D], F32, r_q)
        a1T = at("a1T", [P, KC, D], F32, r_q + 56 * KB)
        yT_hi, yT_lo = at("yT_hi", [P, QH, KC, QW], F32R, r_q), at("yT_lo", [P, QH, KC, QW], F32R, r_q + 16 * KB)
        x_res = at("x_res", [P, QT, D], F32, r_q + 32 * KB)
        yn = at("yn", [P, 4, D], F32, r_q + 48 * KB)
        inv_x = at("inv_x", [P, 2, 4, P], F32, r_q + 56 * KB)
        ks = at("ks", [P, HG, 4, GK], F32R, r_k)
        wfT = at("wfT", [P, KC, D], F32, r_k)
        m12 = at("m12", [P, KC, D], F32, r_k + 8 * KB)
        y_out = at("y_out", [P, 4, D], F32, r_k)
        r_v = region(4 * KB)
        vals = at("vals", [P, GT, D], F32, r_v)
        r_1 = region(16 * KB)
        attn = at("attn", [P, HG, T], F32, r_1)
        xT_lo = at("xT_lo", [P, KC, T], F32R, r_1)
        r_2 = region(16 * KB)
        prob = at("prob", [P, 2, 4, QW], F32, r_2)
        xT_hi = at("xT_hi", [P, KC, T], F32R, r_2)
        r_3 = region(8 * KB)
        q_st = at("q_st", [P, 2, 2, QW], F32R, r_3)
        work = at("work", [P, 4, QW], F32, r_3)
        den_sb, alpha_sb = work[:, 0, :], work[:, 1, :]
        alpha_x = work[:, 2, :].rearrange("p (c n) -> p c n", c=4)
        r_c = region(8 * KB)
        ctx_sb = at("ctx_sb", [P, GT, D], F32, r_c)
        ctxT = at("ctxT", [P, KC, GK], F32, r_c + 4 * KB)
        x_in = at("x_in", [P, 4, D], F32, r_c)
        select = at("select", [P, 4, 8 * DK], F32R, r_c)
        k_st = at("k_st", [P, 2, 2, GK], F32R, r_v)
        ident = own("ident", [P, P])
        bv_b, bo_b, fb_b = own("bv_b", [P, D]), own("bo_b", [P, D]), own("fb_b", [P, D])
        m_run = own("m_run", [P, HG, 4 * QT])
        den_nat = own("den_nat", [P, HG, 4, QT])
        inv_nat = own("inv_nat", [P, HG, 4, QT])
        m_new = own("m_new", [P, 4, QT])
        m_tile = own("m_tile", [P, 4, QT])
        m_pair = own("m_pair", [P, 4, 4 * QT])
        m_dif = own("m_dif", [P, 4, QT])
        alpha_nat = own("alpha_nat", [P, 2, 4, QT])
        mT = own("mT", [2 * 4 * QT, P])
        ones32 = own("ones32", [P, 32])
        bq_c, bk_c = own("bq_c", [P, KC]), own("bk_c", [P, KC])
        stat = own("stat", [P, 4, 6])
        mv = own("mv", [P, 4, 2])
        nw = own("nw", [P, 4, 4])
        nf_all, nf_b = own("nf_all", [P, B]), own("nf_b", [P, 1])
        table = own("table", [1, 116], I32)
        assert top[0] <= 229368, top[0]
        ctl = at("ctl", [1, 2048], F32, r_3)
        mask_sb = at("mask_sb", [B * NT, P], I32, r_v)
        meq = at("meq", [B * NT, P], F32, r_v + 512)
        mbias = at("mbias", [B * NT, P], F32, r_v + 1024)
        flag = at("flag", [B * NT, 1], F32, r_v + 1536)

        ps = es.enter_context(nc.psum_tensor("ps", [P, 8, 512], F32))

        def sem(name):
            return es.enter_context(nc.semaphore(name))

        def sems(names):
            return [sem(n) for n in names.split()]

        ld_small, ld_w = sem("ld_small"), [sem(f"ld_w{n}") for n in range(7)]
        flags_set, flags_stored, flags_row, stack_rows = sems("flags_set flags_stored flags_row stack_rows")
        mask_ready, table_ready, nf_row, nf_ps, constants = sems("mask_ready table_ready nf_row nf_ps constants")
        wt_ps, wt_hi, wt_done, wt_copied, m12_ps, m12_done, wf_ps, wf_h, wf_done = sems(
            "wt_ps wt_hi wt_done wt_copied m12_ps m12_done wf_ps wf_h wf_done")
        x_loaded = [sem(f"x_loaded{n}") for n in range(4)]
        xn_ready, xT_ps, xT_h, xT_l, q_ps, q_h, q_l = sems("xn_ready xT_ps xT_h xT_l q_ps q_h q_l")
        qst_ps, qst_a, qst_d, ones_row = sems("qst_ps qst_a qst_d ones_row")
        ctx_loaded = [sem(f"ctx_loaded{n}") for n in range(GT)]
        ctxT_ps, ctxT_a, ctxT_d, k_ps, k_h, k_l, v_ps, v_done = sems("ctxT_ps ctxT_a ctxT_d k_ps k_h k_l v_ps v_done")
        sel_in, kst_ps, kst_a, kst_d, mask_in = sems("sel_in kst_ps kst_a kst_d mask_in")
        nat0_ps, nat0_done, nat_ps, nat_done, m_ready, m_rows = sems("nat0_ps nat0_done nat_ps nat_done m_ready m_rows")
        s_ps, exp_done, pv_done, den_ps, o_done, den_done = sems("s_ps exp_done pv_done den_ps o_done den_done")
        dif_ready, alpha_exp, alpha_ps, alpha_done = sems("dif_ready alpha_exp alpha_ps alpha_done")
        inv_ready, invx_done, inv_ps, scaled, a_h, a_l, oj_ps, x1_done = sems(
            "inv_ready invx_done inv_ps scaled a_h a_l oj_ps x1_done")
        xr_loaded = [sem(f"xr_loaded{n}") for n in range(QT)]
        xb_done, yn_ready, yT_ps, yT_h, yT_l, f_ps, f_b, f_tanh, y_done = sems(
            "xb_done yn_ready yT_ps yT_h yT_l f_ps f_b f_tanh y_done")
        y_stored = [sem(f"y_stored{n}") for n in range(4)]
        chain = sem("chain")
        PRIMED = 1
        primed = [y_done, f_b, o_done, den_done, nat_done, exp_done, den_ps, alpha_ps, alpha_exp, *y_stored]
        past = {}

        def hold(eng, semaphore, value):
            eng.wait_ge(semaphore, value)
            eng.sem_inc(past[eng], 1)

        PIECES = 2 * QT
        UNITS = QH * GT

        def order():
            todo = [("max", 0, 0), ("values", 0, 0), ("maxT", 0, 0), ("values", 1, 0)]
            for hg in range(HG):
                for u in range(UNITS):
                    now = 4 * hg + u
                    heads = [("scores", now, 0), ("scores", now, 1)]
                    sums = [("weigh", now - 1, 0), ("sum", now - 1, 0)] if now else []
                    items = sums + heads if u == 0 else heads + sums
                    n, start = (((1, 2, 1, 2), 0), ((1, 2, 1, 2), 6), ((1, 2, 1, 0), 12), ((0, 0, 0, 0), 16))[u]
                    for c, item in enumerate(items):
                        todo.append(item)
                        if hg + 1 < HG:
                            take = n[c] if len(items) == 4 else 3
                            todo += [("nat", hg + 1, start + q) for q in range(take)]
                            start += take
                        if u == 3 and item == heads[1] and hg + 1 < HG:
                            todo.append(("maxT", hg + 1, 0))
                        if u % 2 and item == heads[1] and now > 1:
                            todo.append(("denT", (now - 2) // 2, 0))
            todo += [("weigh", 15, 0), ("sum", 15, 0), ("denT", 7, 0)]
            return todo

        ORDER = order()
        TURNS = [item for item in ORDER if item[0] in ("nat", "maxT", "denT")]
        TURN = {item: n for n, item in enumerate(TURNS)}
        NTURN = len(TURNS)
        NAT0_BEFORE = {n: (3 * (n - 2) - (n > 2),) for n in range(2, 8)}
        NAT0_AFTER = {n: (1,) if n == 2 else range(3 * (n - 2), min(3 * (n - 2) + 2, PIECES)) for n in range(2, 8)}
        assert sorted(p for n in range(2, 8) for p in (*NAT0_BEFORE[n], *NAT0_AFTER[n])) == list(range(PIECES))
        F_BANK = (4, 5, 0, 1)
        OUTS = HG * QH
        assert [x for x in ORDER if x[0] == "denT"] == [("denT", w, 0) for w in range(OUTS)]

        def groups(eng, b):
            first = eng.value_load(table[0:1, DS(b, 1)], min_val=0, max_val=B * NT // GT)
            count = eng.value_load(table[0:1, DS(b + 8, 1)], min_val=1, max_val=NT // GT)
            return first, count

        def later(eng, b, i):
            before = eng.value_load(table[0:1, DS(b + 12, 1)], min_val=0, max_val=24)
            return eng.value_load(table[0:1, DS(before + i + 80, 1)], min_val=0, max_val=31)

        def end_group(eng, b):
            return eng.value_load(table[0:1, DS(b + 1, 1)], min_val=1, max_val=B * NT // GT)

        block = es.enter_context(nc.Block())

        @block.sync
        def _(sp):
            past[sp] = sem("sp_past")

            def load_x(nb, t):
                sp.dma_start(x_in[:, t % 4, :], x_rows[DS(nb * T + t * P, P), :]).then_inc(x_loaded[t % 4], 16)

            def load_ctx(tiles):
                for j in range(GT):
                    sp.dma_start(ctx_sb[:, j, :], ctx_rows[DS(tiles[j] * P, P), :]).then_inc(ctx_loaded[j], 16)

            def load_select(k):
                hold(sp, ctxT_ps, k + 1)
                sp.dma_start(select[:, :, :].bitcast(F32), select_dram).then_inc(sel_in, 16)

            def mask_rows_in(tiles):
                for j in range(GT):
                    sp.dma_start(ks[96:97, :, :, j * P:(j + 1) * P].bitcast(F32).rearrange("p a b k -> p (a b) k"),
                                 mbias_dram[DS(tiles[j], 1), :].unsqueeze(1).to_broadcast([1, H, P])).then_inc(mask_in, 16)

            def tiles_of(b, i):
                return [sp.value_load(table[0:1, DS(16 + b * NT + i * GT + j, 1)], min_val=0, max_val=B * NT - 1)
                        for j in range(GT)]

            sp.dma_start(mask_sb[:, :], mask_rows).then_inc(mask_ready, 16)
            sp.dma_start(ident[:, :], ident_in).then_inc(ld_small, 16)
            sp.dma_start(ctl[0:1, 0:NROW], rows_in).then_inc(ld_small, 16)
            for n, w in enumerate((wq, wk, wv, wa1, wa2, wf, wo)):
                sp.dma_start(raw[:, n, :, :], w.rearrange("(r p) c -> p r c", p=P)).then_inc(ld_w[n], 16)
                if n == 0:
                    with nc.allow_non_contiguous_dma(reason="512 words each, once"):
                        sp.dma_start(bq_c[:, :], bq.rearrange("(m p) -> p m", p=P)).then_inc(ld_small, 16)
                        sp.dma_start(bk_c[:, :], bk.rearrange("(m p) -> p m", p=P)).then_inc(ld_small, 16)
                    for dst, src in ((bv_b, bv), (bo_b, bo), (fb_b, fb)):
                        sp.dma_start(dst[:, :], src.partition_broadcast(P)).then_inc(ld_small, 16)
                if n == 2:
                    sp.wait_ge(flags_set, 1)
                    sp.dma_start(mbias_dram, mbias[:, :]).then_inc(flags_stored, 16)
                    sp.dma_start(flags_dram.rearrange("(p a) -> p a", a=1), flag[:, :]).then_inc(flags_stored, 16)
                    sp.wait_ge(flags_stored, 32)
                    sp.dma_start(ctl[0:1, 192:256], flags_dram.rearrange("(a p) -> a p", a=1)).then_inc(flags_row, 16)
                    for t in range(4):
                        load_x(0, t)
            sp.dma_start(ones_dram, ones_in).then_inc(constants, 16)
            sp.dma_start(select_dram, select_in).then_inc(constants, 16)
            for t in range(4, QT):
                sp.wait_ge(xT_ps, t - 3)
                load_x(0, t)
            sp.wait_ge(constants, 32)
            sp.wait_ge(table_ready, 1)
            sp.wait_ge(xT_ps, QT)
            load_ctx(tiles_of(0, 0))
            with sp.Fori(0, B) as b:
                first, count = groups(sp, b)
                load_select(first)
                sp.wait_ge(y_done, b * QT + PRIMED)
                sp.dma_start(qs[96:97, :, :].bitcast(F32).rearrange("p h t -> p (h t)"), ones_dram).then_inc(ones_row, 16)
                tiles = tiles_of(b, 0)
                hold(sp, stack_rows, b + 2)
                mask_rows_in(tiles)
                with sp.Fori(0, count) as i:
                    k = first + i
                    with sp.If(i > 0):
                        load_select(k)
                        tiles = tiles_of(b, i)
                        hold(sp, kst_ps, k * 4 + 1)
                        mask_rows_in(tiles)
                    for hg in range(HG):
                        sp.wait_ge(nat_done, k * NTURN + TURN["maxT", hg, 0] + 1 + PRIMED)
                        for part in range(2):
                            sp.dma_start(qs[97 + part:98 + part, 4 * hg:4 * hg + 4, :].bitcast(F32).rearrange("p a (b c) -> p (a b) c", c=P),
                                         mT[32 * part:32 * part + 32, :]).then_inc(m_rows, 16)
                        if hg == 0:
                            with sp.If(i + 1 < count):
                                hold(sp, kst_ps, k * 4 + 4)
                                load_ctx(tiles_of(b, i + 1))
                last = end_group(sp, b)
                hold(sp, o_done, last * OUTS + PRIMED)
                for t in range(4):
                    sp.dma_start(x_res[:, t, :], x_rows[DS(b * T + t * P, P), :]).then_inc(xr_loaded[t], 16)
                following = sp.value_load(table[0:1, DS(b + 112, 1)], min_val=0, max_val=B - 1)
                with sp.If(b < B - 1):
                    for t in range(4):
                        load_x(following, t)
                for t in range(4, QT):
                    sp.dma_start(x_res[:, t, :], x_rows[DS(b * T + t * P, P), :]).then_inc(xr_loaded[t], 16)

                def store(ts):
                    for t in ts:
                        hold(sp, y_done, b * QT + t + 1 + PRIMED)
                        sp.dma_start(out_rows[DS(b * T + t * P, P), :], y_out[:, t % 4, :]).then_inc(y_stored[t % 4], 16)

                store((0, 1))
                with sp.If(b < B - 1):
                    for t in range(4, QT):
                        hold(sp, xT_ps, b * QT + QT + t - 3)
                        load_x(following, t)
                store((2, 3))
                with sp.If(b < B - 1):
                    tiles = tiles_of(following, 0)
                    hold(sp, xT_ps, b * QT + 2 * QT)
                    load_ctx(tiles)
                store(range(4, QT))
            for n in range(4):
                sp.wait_ge(y_stored[n], B * 32 + PRIMED)

        @block.tensor
        def _(pe):
            past[pe] = sem("pe_past")

            def transposes(out_bank, tile):
                for c in range(KC):
                    last = nc.tensor.transpose(ps[:, out_bank, c * P:(c + 1) * P], tile(c), ident[:, :])
                return last

            def product(out, pairs):
                for kc in range(KC):
                    for n, (left, right) in enumerate(pairs(kc)):
                        last = nc.tensor.matmul(out, left, right, start=kc == 0 and n == 0, stop=kc == KC - 1 and n == 2)
                return last

            def transpose_x(nb, t, free, value):
                pe.wait_ge(xn_ready, nb * QT + t + 1)
                pe.wait_ge(free, value) if t < 2 else pe.wait_ge(xT_l, nb * QT + t - 1)
                transposes(6 + t % 2, lambda c: x_in[:, t % 4, c * P:(c + 1) * P]).then_inc(xT_ps, 1)

            def queries(b, n):
                m, qh = divmod(n, QH)
                cols = slice(m * P, (m + 1) * P)
                a = slice(qh * QW, (qh + 1) * QW)
                if n >= 2:
                    pe.wait_ge(q_l, b * 8 + n - 1)
                product(ps[:, 4 + n % 2, :], lambda kc: ((wq_hi[:, kc, cols], xT_hi[:, kc, a]),
                                                         (wq_hi[:, kc, cols], xT_lo[:, kc, a]),
                                                         (wq_lo[:, kc, cols], xT_hi[:, kc, a]))).then_inc(q_ps, 1)

            def stack_q(b, n, free_a, free_d):
                pe.wait_ge(q_l, b * 8 + n + 1)
                for half, free in enumerate((free_a, free_d)):
                    pe.wait_ge(*free)
                    for s in range(2):
                        for part in range(2):
                            c = Q_PLACES[part] * DK
                            last = nc.tensor.matmul(ps[0:96, (6, 0)[half] + s, :], select[:, 2 * half + s, c:c + 96],
                                                    q_st[:, n % 2, part, :], start=part == 0, stop=part == 1)
                    last.then_inc(qst_ps, 1)

            def context(k):
                for j in range(GT):
                    pe.wait_ge(ctx_loaded[j], k * 16 + 16)
                    last = transposes(j, lambda c: ctx_sb[:, j, c * P:(c + 1) * P])
                last.then_inc(ctxT_ps, 1)

            def keys(k):
                pe.wait_ge(ctxT_a, k + 1)
                pe.wait_ge(ctxT_d, k + 1)
                for m in range(HG):
                    for kc in range(KC):
                        last = nc.tensor.matmul(ps[:, 2 + m // 2, (m % 2) * GK:(m % 2 + 1) * GK],
                                                wkT[:, kc, m * P:(m + 1) * P], ctxT[:, kc, :],
                                                start=kc == 0, stop=kc == KC - 1)
                    if m % 2:
                        last.then_inc(k_ps, 1)

            def scores_by_query(bank, hg, p):
                qt, pair = divmod(p, 2)
                for s in range(2):
                    g = 2 * pair + s
                    last = nc.tensor.matmul(ps[:, bank, s * GK:(s + 1) * GK], qs[0:97, 4 * hg + g, qt * P:(qt + 1) * P],
                                            ks[0:97, hg, g, :], start=True, stop=True)
                return last

            def nat0(b, k, p):
                if p == 0:
                    for stacked in (qst_a, qst_d):
                        pe.wait_ge(stacked, b * 8 + QH)
                    pe.wait_ge(kst_a, k * 2 + 1)
                    pe.wait_ge(mask_in, (k + 1) * 32)
                    pe.wait_ge(ones_row, b * 16 + 16)
                if p >= 2:
                    pe.wait_ge(nat0_done, k * PIECES + p - 1)
                scores_by_query(2 + p % 2, 0, p).then_inc(nat0_ps, 1)

            def stack_k(k, m, free=None):
                if m == 0:
                    pe.wait_ge(sel_in, k * 16 + 16)
                pe.wait_ge(k_l, k * 4 + m + 1)
                if free:
                    pe.wait_ge(*free)
                for g in range(4):
                    for part in range(2):
                        c = K_PLACES[part] * DK
                        last = nc.tensor.matmul(ps[0:96, (6, 0)[m % 2] + g // 2, (g % 2) * GK:(g % 2 + 1) * GK],
                                                select[:, g, c:c + 96], k_st[:, m % 2, part, :], start=part == 0, stop=part == 1)
                last.then_inc(kst_ps, 1)

            pe.wait_ge(ld_small, 16 * 7)
            bank = 0
            for n, earlier in ((0, None), (1, (wt_done, 0)), (2, (wt_copied, 0)), (3, (wt_copied, 4)),
                               (5, (wt_copied, 8)), (6, (wt_copied, 12))):
                pe.wait_ge(ld_w[n], 16)
                for kc in range(KC):
                    if earlier:
                        pe.wait_ge(earlier[0], earlier[1] + kc + 1)
                    transposes(bank % 4, lambda r: raw[:, n, r, kc * P:(kc + 1) * P]).then_inc(wt_ps, 1)
                    bank += 1
                if n == 2:
                    for t in range(4):
                        transpose_x(0, t, ld_small, 16 * 7)
                if n == 5:
                    for t in range(4, QT):
                        transpose_x(0, t, ld_small, 16 * 7)
            pe.wait_ge(wt_done, 2 * KC)
            pe.wait_ge(wt_copied, 4 * KC)
            pe.wait_ge(xT_l, QT)
            pe.wait_ge(ld_w[4], 16)
            for m in range(KC):
                for kc in range(KC):
                    last = nc.tensor.matmul(ps[:, 4 + m, :], a1T[:, kc, m * P:(m + 1) * P], raw[:, 4, kc, :],
                                            start=kc == 0, stop=kc == KC - 1)
                last.then_inc(m12_ps, 1)
            pe.wait_ge(m12_done, KC)
            for m in range(KC):
                for kc in range(KC):
                    last = nc.tensor.matmul(ps[:, 4 + m, :], wfT[:, kc, m * P:(m + 1) * P], m12[:, kc, :],
                                            start=kc == 0, stop=kc == KC - 1)
                last.then_inc(wf_ps, 1)
            pe.wait_ge(nf_row, 1)
            nc.tensor.matmul(ps[:, 0, 0:B], ctl[0:1, 1600:1728], ctl[0:1, 1728:1728 + B], start=True, stop=True).then_inc(nf_ps, 1)
            pe.wait_ge(table_ready, 1)

            with pe.Fori(0, B) as b:
                pe.wait_ge(xT_l, b * QT + QT)
                first, count = groups(pe, b)
                pe.wait_ge(f_b, b * QT + PRIMED)
                context(first)
                queries(b, 0)
                keys(first)
                queries(b, 1)
                stack_k(first, 0)
                stack_k(first, 1)
                stack_q(b, 0, (kst_a, first * 2 + 1), (kst_d, first * 2 + 1))
                queries(b, 2)
                stack_k(first, 2, (qst_a, b * 8 + 1))
                stack_k(first, 3, (qst_d, b * 8 + 1))
                stack_q(b, 1, (kst_a, first * 2 + 2), (kst_d, first * 2 + 2))
                for n in range(2, 8):
                    if n < 7:
                        queries(b, n + 1)
                    for p in NAT0_BEFORE[n]:
                        nat0(b, first, p)
                    stack_q(b, n, (qst_a, b * 8 + n), (qst_d, b * 8 + n))
                    for p in NAT0_AFTER[n]:
                        nat0(b, first, p)
                hold(pe, q_l, b * 8 + 8)
                with pe.Fori(0, count) as i:
                    k = first + i
                    with pe.If(i > 0):
                        context(k)
                        keys(k)
                        pe.wait_ge(o_done, k * OUTS + PRIMED)
                        pe.wait_ge(den_done, k * OUTS + PRIMED)
                        stack_k(k, 0)
                        stack_k(k, 1)
                        stack_k(k, 2, (kst_a, k * 2 + 1))
                        stack_k(k, 3, (kst_d, k * 2 + 1))
                        for p in range(PIECES):
                            nat0(b, k, p)
                    for what, n, p in ORDER:
                        if what in ("nat", "maxT", "denT"):
                            turn = TURN[what, n, p]
                            bank = 4 + turn % 2
                            pe.wait_ge(nat_done, k * NTURN + max(turn - 1, 0) + PRIMED)
                        if what == "nat":
                            scores_by_query(bank, n, p).then_inc(nat_ps, 1)
                        elif what == "values":
                            if n == 0:
                                for stacked in (qst_a, qst_d):
                                    pe.wait_ge(stacked, b * 8 + 8)
                                for stacked in (kst_a, kst_d):
                                    pe.wait_ge(stacked, k * 2 + 2)
                            for kc in range(KC):
                                last = nc.tensor.matmul(ps[:, 6 + n, :], ctxT[:, kc, n * P:(n + 1) * P], wvT[:, kc, :],
                                                        start=kc == 0, stop=kc == KC - 1)
                            last.then_inc(v_ps, 1)
                        elif what == "maxT":
                            pe.wait_ge(m_ready, k * HG + n + 1)
                            nc.tensor.transpose(ps[:, bank, 0:P], m_pair[:, :, :].rearrange("p a b -> p (a b)"),
                                                ident[:, :]).then_inc(nat_ps, 1)
                        elif what == "denT":
                            pe.wait_ge(den_done, k * OUTS + n + 1 + PRIMED)
                            transposes(bank, lambda c: den_sb[:, c * P:(c + 1) * P]).then_inc(nat_ps, 1)
                        elif what == "scores":
                            hg, qh, j = n // 4, n % 4 // GT, n % GT
                            if n % 4 == 0 and p == 0:
                                pe.wait_ge(m_rows, (k * HG + hg + 1) * 32)
                            pe.wait_ge(exp_done, k * 32 + max(2 * n + p - 1, 0) + PRIMED)
                            for s in range(2):
                                g = 2 * p + s
                                last = nc.tensor.matmul(ps[:, 2 * p + s, :], ks[0:99, hg, g, j * P:(j + 1) * P],
                                                        qs[0:99, 4 * hg + g, qh * QW:(qh + 1) * QW],
                                                        start=True, stop=True)
                            last.then_inc(s_ps, 1)
                        elif what == "weigh":
                            j, w = n % GT, n // GT
                            if n == 0:
                                pe.wait_ge(v_done, k * GT + GT)
                            if j == 0:
                                hold(pe, o_done, k * OUTS + w + PRIMED)
                                with pe.If(i > 0):
                                    late = later(pe, b, i)
                                    pe.wait_ge(alpha_exp, late * OUTS + w + 1 + PRIMED)
                                    transposes(6, lambda c: alpha_x[:, c, :]).then_inc(alpha_ps, 1)
                                    hold(pe, alpha_done, late * OUTS + w + 1)
                            pe.wait_ge(exp_done, k * 32 + 2 * n + 2 + PRIMED)
                            for g in range(4):
                                h = 4 * (n // 4) + g
                                last = nc.tensor.matmul(ps[32 * g:32 * g + 32, 6, :], vals[:, j, h * DK:(h + 1) * DK],
                                                        prob[:, n % 2, g, :], start=j == 0, stop=j == GT - 1)
                            last.then_inc(pv_done, 1)
                        elif what == "sum":
                            j, w = n % GT, n // GT
                            if j == 0:
                                pe.wait_ge(den_done, k * OUTS + w + PRIMED)
                            for g in range(4):
                                last = nc.tensor.matmul(ps[32 * g:32 * g + 32, 7, :], ones32[:, :],
                                                        prob[:, n % 2, g, :], start=j == 0, stop=j == GT - 1)
                            last.then_inc(den_ps, 1)

                def inverse(n):
                    pe.wait_ge(invx_done, b * OUTS + n + 1)
                    if n >= 2:
                        pe.wait_ge(scaled, b * OUTS + n - 1)
                    transposes(6 + n % 2, lambda c: inv_x[:, n % 2, c, :]).then_inc(inv_ps, 1)

                def left(t):
                    qh, i = divmod(t, 4)
                    return qh, slice(i * P, (i + 1) * P)

                def out_proj(t):
                    qh, rows = left(t)
                    if t % 4 == 0:
                        pe.wait_ge(a_l, b * OUTS + 4 * qh + 4)
                    if t >= 2:
                        pe.wait_ge(x1_done, b * QT + t - 1)
                    product(ps[:, t % 2, :], lambda kc: ((yT_hi[:, qh, kc, rows], wo_hi[:, kc, :]),
                                                         (yT_hi[:, qh, kc, rows], wo_lo[:, kc, :]),
                                                         (yT_lo[:, qh, kc, rows], wo_hi[:, kc, :]))).then_inc(oj_ps, 1)

                def transpose_y(t):
                    pe.wait_ge(yn_ready, b * QT + t + 1)
                    if t >= 2:
                        pe.wait_ge(yT_l, b * QT + t - 1)
                    transposes(2 + t % 2, lambda c: yn[:, t % 4, c * P:(c + 1) * P]).then_inc(yT_ps, 1)

                def ffn(t):
                    qh, rows = left(t)
                    pe.wait_ge(yT_l, b * QT + t + 1)
                    if t >= 4:
                        pe.wait_ge(f_b, b * QT + t - 3 + PRIMED)
                    elif t == 2:
                        pe.wait_ge(x1_done, b * QT + QT)
                    product(ps[:, F_BANK[t % 4], :], lambda kc: ((yT_hi[:, qh, kc, rows], wf_hi[:, kc, :]),
                                                             (yT_hi[:, qh, kc, rows], wf_lo[:, kc, :]),
                                                             (yT_lo[:, qh, kc, rows], wf_hi[:, kc, :]))).then_inc(f_ps, 1)

                def next_x(half):
                    with pe.If(b < B - 1):
                        for t in range(4 * half, 4 * half + 4):
                            transpose_x(b + 1, t, scaled, b * OUTS + OUTS)

                for n in range(4):
                    inverse(n)
                for t in range(4):
                    out_proj(t)
                    inverse(4 + t)
                for t in range(4, QT):
                    out_proj(t)
                for t in range(4):
                    transpose_y(t)
                ffn(0)
                ffn(1)
                for t in range(4, QT):
                    transpose_y(t)
                for t in range(2, 6):
                    ffn(t)
                next_x(0)
                ffn(6)
                ffn(7)
                next_x(1)

        @block.scalar
        def _(act):
            def high_x(nb, t):
                act.wait_ge(xT_ps, nb * QT + t + 1)
                nc.scalar.activation(xT_hi[:, :, t * P:(t + 1) * P], ps[:, 6 + t % 2, :].rearrange("p (a c) -> p a c", c=P),
                                     ACT.Copy).then_inc(xT_h, 1)

            def high_q(b, n):
                act.wait_ge(q_ps, b * 8 + n + 1)
                if n >= 2:
                    act.wait_ge(qst_ps, b * 16 + 2 * n - 2)
                nc.scalar.activation(q_st[:, n % 2, 0, :], ps[:, 4 + n % 2, :], ACT.Identity,
                                     bias=bq_c[:, n // 2:n // 2 + 1]).then_inc(q_h, 1)

            def copy_q(b, n):
                act.wait_ge(qst_ps, b * 16 + 2 * n + 1)
                nc.scalar.activation(qs[0:96, 4 * (n // 2):4 * (n // 2) + 2, (n % 2) * QW:(n % 2 + 1) * QW], ps[0:96, 6:8, :],
                                     ACT.Copy).then_inc(qst_a, 1)

            def high_c(k):
                act.wait_ge(ctxT_ps, k + 1)
                nc.scalar.activation(ctxT[:, :, 0:P], ps[:, 0, :].rearrange("p (a c) -> p a c", c=P), ACT.Copy).then_inc(ctxT_a, 1)

            def high_k(k, half):
                act.wait_ge(k_ps, k * 2 + half + 1)
                for m in (2 * half, 2 * half + 1):
                    if half:
                        act.wait_ge(kst_ps, k * 4 + m - 1)
                    nc.scalar.activation(k_st[:, m % 2, 0, :], ps[:, 2 + half, (m % 2) * GK:(m % 2 + 1) * GK],
                                         ACT.Identity, bias=bk_c[:, m:m + 1]).then_inc(k_h, 1)

            def copy_k(k, m):
                act.wait_ge(kst_ps, k * 4 + m + 1)
                nc.scalar.activation(ks[0:96, m, :, :].rearrange("p b k -> p (b k)"),
                                     ps[0:96, 6:8, :].rearrange("p a k -> p (a k)"), ACT.Copy).then_inc(kst_a, 1)

            bank = 0
            for n in (0, 1, 2, 3, 5, 6):
                for kc in range(KC):
                    act.wait_ge(wt_ps, bank + 1)
                    if n in (1, 2, 3, 5):
                        nc.scalar.activation({1: wkT, 2: wvT, 3: a1T, 5: wfT}[n][:, kc, :], ps[:, bank % 4, :],
                                             ACT.Copy).then_inc(wt_copied, 1)
                    else:
                        nc.scalar.activation((wq_hi if n == 0 else wo_hi)[:, kc, :], ps[:, bank % 4, :], ACT.Copy).then_inc(wt_hi, 1)
                    bank += 1
                if n in (2, 5):
                    for t in range(4 * (n == 5), 4 * (n == 5) + 4):
                        high_x(0, t)
            for m in range(KC):
                act.wait_ge(m12_ps, m + 1)
                nc.scalar.activation(m12[:, m, :], ps[:, 4 + m, :], ACT.Copy).then_inc(m12_done, 1)
            for m in range(KC):
                act.wait_ge(wf_ps, m + 1)
                nc.scalar.activation(wf_hi[:, m, :], ps[:, 4 + m, :], ACT.Copy).then_inc(wf_h, 1)
            act.wait_ge(table_ready, 1)
            act.wait_ge(ld_small, 16 * 7)

            with act.Fori(0, B) as b:
                first, count = groups(act, b)
                high_c(first)
                high_q(b, 0)
                high_k(first, 0)
                high_q(b, 1)
                act.wait_ge(stack_rows, b + 2)
                copy_k(first, 0)
                high_k(first, 1)
                act.wait_ge(y_done, b * QT + PRIMED)
                copy_q(b, 0)
                high_q(b, 2)
                copy_k(first, 2)
                copy_q(b, 1)
                for n in range(2, 8):
                    if n < 7:
                        high_q(b, n + 1)
                    copy_q(b, n)
                with act.Fori(0, count) as i:
                    k = first + i
                    with act.If(i > 0):
                        high_c(k)
                        high_k(k, 0)
                        copy_k(k, 0)
                        high_k(k, 1)
                        copy_k(k, 2)
                    for what, n, p in ORDER:
                        if what == "scores":
                            hg, w = n // 4, n // GT
                            if n % GT == 0 and p == 0:
                                with act.If(i > 0):
                                    late = later(act, b, i)
                                    act.wait_ge(dif_ready, late * HG + hg + 1)
                                    act.wait_ge(alpha_ps, late * OUTS + w + PRIMED)
                                    if w % QH == 0:
                                        nc.scalar.activation(alpha_nat[:, hg % 2, :, :], m_dif[:, :, :], ACT.Exp, scale=SCALE)
                                    for c in range(4):
                                        qt = 4 * (w % QH) + c
                                        last = nc.scalar.activation(
                                            alpha_x[:, c, :].rearrange("p (g r) -> p g r", r=32),
                                            m_dif[:, :, qt:qt + 1].to_broadcast([P, 4, 32]), ACT.Exp, scale=SCALE)
                                    last.then_inc(alpha_exp, 1)
                            act.wait_ge(s_ps, k * 32 + 2 * n + p + 1)
                            act.wait_ge(den_ps, k * 16 + max(n - 1, 0) + PRIMED)
                            nc.scalar.activation(prob[:, n % 2, 2 * p:2 * p + 2, :], ps[:, 2 * p:2 * p + 2, :],
                                                 ACT.Exp, scale=SCALE).then_inc(exp_done, 1)
                        elif what == "sum" and n % GT == GT - 1:
                            w = n // GT
                            act.wait_ge(den_ps, k * 16 + n + 1 + PRIMED)
                            if w:
                                act.wait_ge(nat_ps, k * NTURN + TURN["denT", w - 1, 0] + 1)
                            nc.scalar.activation(den_sb, ps[:, 7, :], ACT.Copy).then_inc(den_done, 1)

                def spread(n):
                    qh, hg = divmod(n, 4)
                    if n == 0:
                        act.wait_ge(inv_ready, b + 1)
                    if n >= 2:
                        act.wait_ge(inv_ps, b * OUTS + n - 1)
                    nc.scalar.activation(inv_x[:, n % 2, :, :].rearrange("p c (g r) -> p c g r", r=32),
                                         inv_nat[:, hg, :, 4 * qh:4 * qh + 4].rearrange("p g c -> p c g").unsqueeze(3).to_broadcast([P, 4, 4, 32]),
                                         ACT.Copy).then_inc(invx_done, 1)

                def high_a(n):
                    qh, hg = divmod(n, 4)
                    act.wait_ge(scaled, b * OUTS + n + 1)
                    nc.scalar.activation(yT_hi[:, qh, hg, :], attn[:, hg, qh * QW:(qh + 1) * QW], ACT.Copy).then_inc(a_h, 1)

                def high_y(t):
                    act.wait_ge(yT_ps, b * QT + t + 1)
                    nc.scalar.activation(yT_hi[:, t // 4, :, (t % 4) * P:(t % 4 + 1) * P],
                                         ps[:, 2 + t % 2, :].rearrange("p (a c) -> p a c", c=P), ACT.Copy).then_inc(yT_h, 1)

                def tanh(t):
                    act.wait_ge(f_b, b * QT + t + 1 + PRIMED)
                    nc.scalar.activation(y_out[:, t % 4, :], y_out[:, t % 4, :], ACT.Tanh).then_inc(f_tanh, 1)

                def next_x(half):
                    with act.If(b < B - 1):
                        for t in range(4 * half, 4 * half + 4):
                            high_x(b + 1, t)

                spread(0)
                spread(1)
                for n in range(OUTS):
                    high_a(n)
                    if n + 2 < OUTS:
                        spread(n + 2)
                for t in range(4):
                    high_y(t)
                tanh(0)
                for t in range(4, QT):
                    high_y(t)
                for t in range(1, 6):
                    tanh(t)
                next_x(0)
                tanh(6)
                tanh(7)
                next_x(1)

        @block.gpsimd
        def _(pool):
            past[pool] = sem("pool_past")
            for semaphore in primed:
                pool.sem_inc(semaphore, PRIMED)
            pool.wait_ge(wf_ps, KC)
            nc.gpsimd.memset(ks[96:P, 2:HG, :, :].bitcast(F32), -1.0).then_inc(stack_rows, 1)
            with pool.Fori(0, B) as b:
                for n in range(4):
                    hold(pool, y_stored[n], b * 32 + PRIMED)
                nc.gpsimd.memset(ks[96:P, 0:2, :, :].bitcast(F32), -1.0).then_inc(stack_rows, 1)
                for t in range(QT):
                    pool.wait_ge(xr_loaded[t], b * 16 + 16)
                    nc.gpsimd.tensor_tensor(x_res[:, t, :], x_res[:, t, :], bo_b[:, :], ALU.add).then_inc(xb_done, 1)
                for t in range(QT):
                    pool.wait_ge(f_tanh, b * QT + t + 1)
                    nc.gpsimd.tensor_tensor(y_out[:, t % 4, :], y_out[:, t % 4, :], x_res[:, t, :], ALU.add).then_inc(y_done, 1)

        @block.vector
        def _(dve):
            past[dve] = sem("dve_past")
            links = [0]

            def link(ins):
                links[0] += 1
                ins.then_inc(chain, 1)
                dve.wait_ge(chain, links[0])

            def cut():
                links[0] = 0
                dve.sem_clear(chain)

            V = nc.vector

            dve.wait_ge(mask_ready, 16)
            link(V.tensor_scalar(meq[:, :], mask_sb[:, :], 0.0, None, ALU.is_equal))
            V.tensor_scalar(mbias[:, :], meq[:, :], MASKED, None, ALU.mult)
            link(V.tensor_reduce(flag[:, :], meq[:, :], AX, ALU.min))
            V.memset(ones32[:, :], 1.0)
            V.memset(ctl[0:1, 1600:1728], 1.0).then_inc(flags_set, 1)

            def low_weights(n, lo, hi):
                for kc in range(KC):
                    dve.wait_ge(wt_hi, n * KC + kc + 1)
                    V.tensor_tensor(lo[:, kc, :], ps[:, kc, :], hi[:, kc, :].bitcast(F32), ALU.subtract).then_inc(wt_done, 1)

            def newton():
                a, y, t_, n_ = (nw[:, q, :] for q in range(4))
                link(V.tensor_scalar(a, mv[:, :, 1], EPS, None, ALU.add))
                link(V.tensor_scalar(n_.bitcast(I32), a.bitcast(I32), 1, None, ALU.arith_shift_right))
                link(V.tensor_scalar(y.bitcast(I32), n_.bitcast(I32), -1.0, float(0x5F3759DF), ALU.mult, ALU.add))
                for _ in range(3):
                    link(V.scalar_tensor_tensor(t_, y, -0.5, y, ALU.mult, ALU.mult))
                    link(V.tensor_tensor(t_, t_, a, ALU.mult))
                    link(V.scalar_tensor_tensor(y, t_, 1.5, y, ALU.add, ALU.mult))

            def moments(last):
                link(last)
                for i in range(4):
                    last = V.bn_aggr(mv[:, i, :], stat[:, i, :])
                link(last)
                newton()

            def norm_x(nb, half):
                for i in range(4):
                    dve.wait_ge(x_loaded[i], (nb * 2 + half + 1) * 16)
                    last = V.bn_stats(stat[:, i, :], x_in[:, i, :])
                moments(last)
                for i in range(4):
                    V.tensor_scalar(x_in[:, i, :], x_in[:, i, :], mv[:, i, 0:1], nw[:, 1, i:i + 1],
                                    ALU.subtract, ALU.mult).then_inc(xn_ready, 1)

            def low_x(nb, half):
                for t in range(4 * half, 4 * half + 4):
                    dve.wait_ge(xT_h, nb * QT + t + 1)
                    cols = slice(t * P, (t + 1) * P)
                    V.tensor_tensor(xT_lo[:, :, cols], ps[:, 6 + t % 2, :].rearrange("p (a c) -> p a c", c=P),
                                    xT_hi[:, :, cols].bitcast(F32), ALU.subtract).then_inc(xT_l, 1)

            def low_q(b, n):
                dve.wait_ge(q_h, b * 8 + n + 1)
                V.scalar_tensor_tensor(q_st[:, n % 2, 1, :], ps[:, 4 + n % 2, :], bq_c[:, n // 2:n // 2 + 1],
                                       q_st[:, n % 2, 0, :].bitcast(F32), ALU.add, ALU.subtract).then_inc(q_l, 1)

            def copy_q(b, n):
                dve.wait_ge(qst_ps, b * 16 + 2 * n + 2)
                V.tensor_copy(qs[0:96, 4 * (n // 2) + 2:4 * (n // 2) + 4, (n % 2) * QW:(n % 2 + 1) * QW],
                              ps[0:96, 0:2, :]).then_inc(qst_d, 1)

            def reduce_nat0(k, p):
                qt, pair = divmod(p, 2)
                dve.wait_ge(nat0_ps, k * PIECES + p + 1)
                V.tensor_reduce(m_tile[:, 2 * pair:2 * pair + 2, qt:qt + 1].rearrange("p a b -> p (a b)"),
                                ps[:, 2 + p % 2, :].rearrange("p (a c) -> p a c", c=GK), AX, ALU.max).then_inc(nat0_done, 1)

            def low_c(k):
                dve.wait_ge(ctxT_ps, k + 1)
                V.tensor_copy(ctxT[:, :, P:2 * P], ps[:, 1, :].rearrange("p (a c) -> p a c", c=P)).then_inc(ctxT_d, 1)

            def low_k(k, half):
                dve.wait_ge(k_h, k * HG + 2 * half + 2)
                for m in (2 * half, 2 * half + 1):
                    V.scalar_tensor_tensor(k_st[:, m % 2, 1, :], ps[:, 2 + half, (m % 2) * GK:(m % 2 + 1) * GK],
                                           bk_c[:, m:m + 1], k_st[:, m % 2, 0, :].bitcast(F32), ALU.add, ALU.subtract).then_inc(k_l, 1)

            def copy_k(k, m):
                dve.wait_ge(kst_ps, k * 4 + m + 1)
                V.tensor_copy(ks[0:96, m, :, :].rearrange("p b k -> p (b k)"),
                              ps[0:96, 0:2, :].rearrange("p a k -> p (a k)")).then_inc(kst_d, 1)

            low_weights(0, wq_lo, wq_hi)
            norm_x(0, 0)
            low_x(0, 0)
            norm_x(0, 1)
            low_x(0, 1)
            low_weights(1, wo_lo, wo_hi)
            dve.wait_ge(flags_row, 16)
            dve.wait_ge(ld_small, 16 * 7)
            tno, b16 = ctl[0:1, 0:64], ctl[0:1, 64:128]
            ev, low = ctl[0:1, 128:136], ctl[0:1, 136:156]
            e, key, rank = ctl[0:1, 192:256], ctl[0:1, 256:320], ctl[0:1, 320:384]
            perm, n_act, grp, gt8 = ctl[0:1, 384:448], ctl[0:1, 448:452], ctl[0:1, 456:460], ctl[0:1, 464:496]
            act_t, cum5, acc, val = ctl[0:1, 1536:1600], ctl[0:1, 1760:1780], ctl[0:1, 1784:1789], ctl[0:1, 1792:1796]
            cmp4 = ctl[0:1, 512:1536].rearrange("p (b t u) -> p b t u", b=B, t=NT)
            link(V.scalar_tensor_tensor(key, e, float(NT), tno, ALU.mult, ALU.add))
            k3 = key.rearrange("p (b t) -> p b t", b=B)
            link(V.tensor_tensor(cmp4, k3.unsqueeze(2).to_broadcast([1, B, NT, NT]),
                                 k3.unsqueeze(3).to_broadcast([1, B, NT, NT]), ALU.is_lt))
            link(V.tensor_reduce(rank.rearrange("p (b t) -> p b t", b=B), cmp4, AX, ALU.add))
            r3 = rank.rearrange("p (b t) -> p b t", b=B)
            t3 = tno.rearrange("p (b t) -> p b t", b=B)
            link(V.tensor_tensor(cmp4, r3.unsqueeze(2).to_broadcast([1, B, NT, NT]),
                                 t3.unsqueeze(3).to_broadcast([1, B, NT, NT]), ALU.is_equal))
            link(V.tensor_tensor(cmp4, cmp4, t3.unsqueeze(2).to_broadcast([1, B, NT, NT]), ALU.mult))
            link(V.tensor_reduce(perm.rearrange("p (b t) -> p b t", b=B), cmp4, AX, ALU.add))
            V.tensor_tensor(table[0:1, 16:80], perm, b16, ALU.add)
            link(V.tensor_scalar(act_t, e, -1.0, 1.0, ALU.mult, ALU.add))
            link(V.tensor_reduce(n_act, act_t.rearrange("p (b t) -> p b t", b=B), AX, ALU.add))
            g3 = gt8.rearrange("p (b i) -> p b i", b=B)
            link(V.tensor_tensor(g3, n_act.unsqueeze(2).to_broadcast([1, B, 8]), ev.unsqueeze(1).to_broadcast([1, B, 8]), ALU.is_gt))
            link(V.tensor_reduce(grp, g3, AX, ALU.add))
            link(V.tensor_scalar(grp, grp, 1.0, None, ALU.max))
            V.tensor_copy(table[0:1, 8:12], grp)
            c3 = cum5.rearrange("p (j b) -> p j b", b=B)
            link(V.tensor_tensor(c3, grp.unsqueeze(1).to_broadcast([1, B + 1, B]), low.rearrange("p (j b) -> p j b", b=B), ALU.mult))
            link(V.tensor_reduce(acc, c3, AX, ALU.add))
            V.tensor_copy(table[0:1, 80:112], ctl[0:1, 160:192])
            V.tensor_scalar(table[0:1, 112:116], ctl[0:1, 156:160], 1.0, B - 1.0, ALU.add, ALU.min)
            V.tensor_tensor(table[0:1, 12:16], acc[:, 0:4], ctl[0:1, 156:160], ALU.subtract)
            link(V.tensor_copy(table[0:1, 0:5], acc))
            link(V.tensor_scalar(val, n_act, 1.0, None, ALU.min))
            link(V.reciprocal(ctl[0:1, 1740:1744], val))
            V.tensor_tensor(ctl[0:1, 1728:1732], val, ctl[0:1, 1740:1744], ALU.mult).then_inc(nf_row, 1)

            for m in range(KC):
                dve.wait_ge(wf_h, m + 1)
                V.tensor_tensor(wf_lo[:, m, :], ps[:, 4 + m, :], wf_hi[:, m, :].bitcast(F32), ALU.subtract).then_inc(wf_done, 1)
            dve.wait_ge(nf_ps, 1)
            link(V.tensor_copy(nf_all[:, :], ps[:, 0, 0:B]))
            cut()
            V.memset(m_pair[:, :, :], 0.0).then_inc(table_ready, 1)

            with dve.Fori(0, B) as b:
                V.memset(m_run[:, :, :], LOWEST)
                V.memset(den_nat[:, :, :, :], 0.0)
                link(V.tensor_copy(nf_b[:, :], nf_all[:, DS(b, 1)]))
                cut()
                first, count = groups(dve, b)
                low_c(first)
                low_q(b, 0)
                low_k(first, 0)
                low_q(b, 1)
                dve.wait_ge(stack_rows, b + 2)
                copy_k(first, 1)
                low_k(first, 1)
                dve.wait_ge(y_done, b * QT + PRIMED)
                copy_q(b, 0)
                low_q(b, 2)
                copy_k(first, 3)
                copy_q(b, 1)
                for n in range(2, 8):
                    if n < 7:
                        low_q(b, n + 1)
                    for p in NAT0_BEFORE[n]:
                        reduce_nat0(first, p)
                    copy_q(b, n)
                    for p in NAT0_AFTER[n]:
                        reduce_nat0(first, p)
                with dve.Fori(0, count) as i:
                    k = first + i

                    def maxima(hg):
                        if hg:
                            dve.wait_ge(nat_done, k * NTURN + TURN["nat", hg, PIECES - 1] + 1 + PRIMED)
                        else:
                            dve.wait_ge(nat0_done, (k + 1) * PIECES)
                        run = m_run[:, hg, :].rearrange("p (a b) -> p a b", b=QT)
                        link(V.tensor_tensor(m_new[:, :, :], m_tile[:, :, :], run, ALU.max))
                        with dve.If(i > 0):
                            late = later(dve, b, i)
                            dve.wait_ge(alpha_exp, late * OUTS + hg * QH + PRIMED)
                            V.tensor_tensor(m_dif[:, :, :], run, m_new[:, :, :], ALU.subtract).then_inc(dif_ready, 1)
                            hold(dve, dif_ready, late * HG + hg + 1)
                        V.tensor_copy(run, m_new[:, :, :])
                        hi, lo = m_pair[:, 0, :], m_pair[:, 1, :]
                        new = m_new[:, :, :].rearrange("p a b -> p (a b)")
                        link(V.tensor_copy(hi.bitcast(F32R), new))
                        V.tensor_tensor(lo, new, hi, ALU.subtract).then_inc(m_ready, 1)
                        cut()

                    with dve.If(i > 0):
                        low_c(k)
                        low_k(k, 0)
                        copy_k(k, 1)
                        low_k(k, 1)
                        copy_k(k, 3)
                        for p in range(PIECES):
                            reduce_nat0(k, p)
                    for what, n, p in ORDER:
                        if what in ("nat", "maxT", "denT"):
                            turn = TURN[what, n, p]
                            src = ps[:, 4 + turn % 2, :]
                        if what in ("nat", "maxT"):
                            dve.wait_ge(nat_ps, k * NTURN + turn + 1)
                        if what == "nat":
                            qt, pair = divmod(p, 2)
                            V.tensor_reduce(m_tile[:, 2 * pair:2 * pair + 2, qt:qt + 1].rearrange("p a b -> p (a b)"),
                                            src.rearrange("p (a c) -> p a c", c=GK), AX, ALU.max).then_inc(nat_done, 1)
                            if p == PIECES - 1:
                                maxima(n)
                        elif what == "max":
                            maxima(0)
                        elif what == "values":
                            dve.wait_ge(v_ps, k * GT + n + 1)
                            V.tensor_tensor(vals[:, n, :], ps[:, 6 + n, :], bv_b[:, :], ALU.add).then_inc(v_done, 1)
                        elif what == "maxT":
                            if n:
                                dve.wait_ge(m_rows, (k * HG + n) * 32)
                            V.tensor_copy(mT[:, :], src[0:64, 0:P]).then_inc(nat_done, 1)
                        elif what == "denT":
                            hg, qh = divmod(n, QH)
                            den = den_nat[:, hg, :, 4 * qh:4 * qh + 4]
                            hold(dve, nat_ps, k * NTURN + turn + 1)
                            with dve.If(i > 0):
                                V.tensor_tensor(den, den, alpha_nat[:, hg % 2, :, 4 * qh:4 * qh + 4], ALU.mult).then_inc(chain, 1)
                                dve.wait_ge(chain, 1)
                                dve.sem_clear(chain)
                            V.tensor_tensor(den, src.rearrange("p (c g r) -> p g c r", c=4, r=32)[:, :, :, 0], den,
                                            ALU.add).then_inc(nat_done, 1)
                        elif what == "weigh" and n % GT == 0:
                            with dve.If(i > 0):
                                late = later(dve, b, i)
                                dve.wait_ge(alpha_ps, late * OUTS + n // GT + 1 + PRIMED)
                                V.tensor_copy(alpha_sb, ps[:, 6, :]).then_inc(alpha_done, 1)
                        elif what == "weigh":
                            w = n // GT
                            hg, qh = divmod(w, QH)
                            dst = attn[:, hg, qh * QW:(qh + 1) * QW]
                            hold(dve, pv_done, k * 16 + n + 1)
                            with dve.If(i > 0):
                                V.tensor_tensor(dst, dst, alpha_sb, ALU.mult).then_inc(chain, 1)
                                dve.wait_ge(chain, 1)
                                dve.sem_clear(chain)
                                V.tensor_tensor(dst, ps[:, 6, :], dst, ALU.add).then_inc(o_done, 1)
                            with dve.If(i < 1):
                                V.tensor_copy(dst, ps[:, 6, :]).then_inc(o_done, 1)

                def scale_a(n):
                    qh, hg = divmod(n, 4)
                    dst = attn[:, hg, qh * QW:(qh + 1) * QW]
                    dve.wait_ge(inv_ps, b * OUTS + n + 1)
                    V.tensor_tensor(dst, ps[:, 6 + n % 2, :], dst, ALU.mult).then_inc(scaled, 1)

                def low_a(n):
                    qh, hg = divmod(n, 4)
                    dve.wait_ge(a_h, b * OUTS + n + 1)
                    V.tensor_tensor(yT_lo[:, qh, hg, :], attn[:, hg, qh * QW:(qh + 1) * QW], yT_hi[:, qh, hg, :].bitcast(F32),
                                    ALU.subtract).then_inc(a_l, 1)

                def residual(t):
                    dve.wait_ge(oj_ps, b * QT + t + 1)
                    dve.wait_ge(xb_done, b * QT + t + 1)
                    V.tensor_tensor(x_res[:, t, :], ps[:, t % 2, :], x_res[:, t, :], ALU.add).then_inc(x1_done, 1)
                    dve.wait_ge(x1_done, b * QT + t + 1)
                    return V.bn_stats(stat[:, t % 4, :], x_res[:, t, :])

                def norm_y(half, last):
                    moments(last)
                    for t in range(4 * half, 4 * half + 4):
                        if half:
                            dve.wait_ge(yT_ps, b * QT + t - 3)
                        V.tensor_scalar(yn[:, t % 4, :], x_res[:, t, :], mv[:, t % 4, 0:1], nw[:, 1, t % 4:t % 4 + 1],
                                        ALU.subtract, ALU.mult).then_inc(yn_ready, 1)

                def low_y(t):
                    dve.wait_ge(yT_h, b * QT + t + 1)
                    cols = slice((t % 4) * P, (t % 4 + 1) * P)
                    V.tensor_tensor(yT_lo[:, t // 4, :, cols], ps[:, 2 + t % 2, :].rearrange("p (a c) -> p a c", c=P),
                                    yT_hi[:, t // 4, :, cols].bitcast(F32), ALU.subtract).then_inc(yT_l, 1)

                def ffn_bias(t):
                    dve.wait_ge(f_ps, b * QT + t + 1)
                    dve.wait_ge(y_stored[t % 4], (2 * b + t // 4) * 16 + PRIMED)
                    V.tensor_tensor(y_out[:, t % 4, :], ps[:, F_BANK[t % 4], :], fb_b[:, :], ALU.add).then_inc(f_b, 1)

                def next_x(norm, low):
                    with dve.If(b < B - 1):
                        if norm is not None:
                            norm_x(b + 1, norm)
                            cut()
                        if low is not None:
                            low_x(b + 1, low)

                hold(dve, nat_done, end_group(dve, b) * NTURN + PRIMED)
                link(V.reciprocal(inv_nat[:, :, :, :], den_nat[:, :, :, :]))
                V.tensor_scalar(inv_nat[:, :, :, :], inv_nat[:, :, :, :], nf_b[:, 0:1], None, ALU.mult).then_inc(inv_ready, 1)
                for n in range(4):
                    scale_a(n)
                    if n:
                        low_a(n - 1)
                low_a(3)
                for t in range(4):
                    last = residual(t)
                    scale_a(4 + t)
                    low_a(4 + t)
                norm_y(0, last)
                for t in range(4, QT):
                    last = residual(t)
                for t in range(4):
                    low_y(t)
                norm_y(1, last)
                cut()
                ffn_bias(0)
                for t in range(4, QT):
                    low_y(t)
                ffn_bias(1)
                next_x(0, None)
                for t in range(2, 6):
                    ffn_bias(t)
                next_x(None, 0)
                next_x(1, None)
                ffn_bias(6)
                ffn_bias(7)
                next_x(None, 1)


_INS = ['x', 'ctx_1024', 'mask_Bx1x1xS2_ik0', 'L0_xattn_W_q', 'L0_xattn_b_q', 'L0_xattn_W_k', 'L0_xattn_b_k',
        'L0_xattn_W_v', 'L0_xattn_b_v', 'L0_xattn_W_o', 'L0_xattn_b_o', 'L0_ffn_weight', 'L0_ffn_aux_weight1',
        'L0_ffn_aux_weight2', 'L0_ffn_bias']


def kernel(**inputs):
    import numpy as _np
    import concourse.bacc as _bacc
    from concourse import mybir as _mybir
    from concourse.bass_utils import run_bass_kernel_spmd as _run

    nc = _bacc.Bacc("TRN2", target_bir_lowering=False, num_devices=1)
    arrays, args = {}, []
    given = [(n, _np.ascontiguousarray(inputs[n])) for n in _INS]
    given += [("identity", _np.eye(P, dtype=_np.float32)), ("selections", selections()), ("ones", _np.ones((1, H * T), _np.float32)),
              ("control_rows", control_constants())]
    for name, a in given:
        arrays[f"in_{name}"] = a
        args.append(nc.dram_tensor(f"in_{name}", a.shape, _mybir.dt.from_np(a.dtype), kind="ExternalInput").ap())
    out = nc.dram_tensor("out_0", (B, T, D), _mybir.dt.float32, kind="ExternalOutput").ap()
    build(nc, *args, out)
    r = _run(nc, [arrays], core_ids=[0])
    return r.results[0]["out_0"]
```
